# Optimizing a Trainium2 kernel written in Bass

```python
import numpy as np
import jax
import jax.numpy as jnp

def _softmax(x, axis=-1):
    return jax.nn.softmax(x, axis=axis)

def _gelu(x):
    return jax.nn.gelu(x, approximate=True)

def _silu(x):
    return jax.nn.silu(x)

def _sigmoid(x):
    return jax.nn.sigmoid(x)

def _layernorm(x, axis=-1, eps=1e-05):
    m = jnp.mean(x, axis=axis, keepdims=True)
    v = jnp.var(x, axis=axis, keepdims=True)
    return (x - m) / jnp.sqrt(v + eps)

def _scatter_add(tgt, idx, src, axis=0):
    return tgt.at[idx].add(src)

def _segment_sum(src, seg, n):
    return jax.ops.segment_sum(src, seg, n)
kernel_name = 'mk_adj_preln_d4_adj_r2_94daf9'

def setup_inputs(seed: int=0):
    np.random.seed(seed)
    _w = jnp.asarray

    def _rec_inputs():
        import jax
        import jax.numpy as jnp
        _gk = jax.random.key(seed)
        x = -0.0003929 + 0.9999 * jax.random.normal(jax.random.fold_in(_gk, 1), (32, 256, 512), jnp.float32)
        _w = (1.0 + jnp.arange(256, dtype=jnp.float32)) ** (-0.5)
        _w = _w / _w.mean()
        _pij = jnp.clip(0.015625 * _w[:, None] * _w[None, :], 0.0, 1.0)
        _a = jax.random.uniform(jax.random.fold_in(_gk, 2), (256, 256)) < _pij
        _a = jnp.logical_or(_a, jnp.swapaxes(_a, -1, -2))
        _a = jnp.logical_or(_a, jnp.eye(256, dtype=bool))
        _af = _a.astype(jnp.float32)
        _af = _af * jax.random.uniform(jax.random.fold_in(_gk, 3), (256, 256), jnp.float32, 0.05, 0.198159)
        adj = _af
        return (x, adj)
    x, adj = _rec_inputs()

    def _L0_gnn_setup():
        import jax, jax.numpy as jnp
        import numpy as np
        NEG_SLOPE = 0.01
        key = jax.random.key(seed)
        k1, k2, k3, k4, k5 = jax.random.split(key, 5)
        B, C, N, O = (32, 256, 512, 256)
        x = jax.random.normal(k1, (B, C, N), dtype=jnp.float32)
        wq = jax.random.normal(k2, (C,), dtype=jnp.float32) * (1.0 / np.sqrt(C))
        wk = jax.random.normal(k3, (C,), dtype=jnp.float32) * (1.0 / np.sqrt(C))
        wm = jax.random.normal(k4, (O, C), dtype=jnp.float32) * (1.0 / np.sqrt(C))
        bm = jax.random.normal(k5, (O,), dtype=jnp.float32) * 0.01
        return {'x': x, 'wq': wq, 'wk': wk, 'wm': wm, 'bm': bm}
    _L0_gnn_all = _L0_gnn_setup()
    _L0_gnn_in = {k: v for k, v in _L0_gnn_all.items() if k in ('wq', 'wk', 'bm')}
    del _L0_gnn_all

    def _L1_gnn_setup():
        import jax, jax.numpy as jnp
        import numpy as np
        EPS = 1e-08

        def _row_stochastic_causal(A, causal_mask):
            A = A * causal_mask
            deg = jnp.maximum(A.sum(axis=-1, keepdims=True), EPS)
            return A / deg
        key = jax.random.key(seed)
        k = jax.random.split(key, 5)
        B, N, D = (4, 1024, 512)
        s = 1.0 / np.sqrt(D)
        h = jax.random.normal(k[0], (B, N, D), dtype=jnp.float32)
        W_lang = jax.random.normal(k[1], (D, D), dtype=jnp.float32) * s
        W_grav = jax.random.normal(k[2], (D, D), dtype=jnp.float32) * s
        W_V = jax.random.normal(k[3], (D, D), dtype=jnp.float32) * s
        W_O = jax.random.normal(k[4], (D, D), dtype=jnp.float32) * s
        causal_mask = jnp.tril(jnp.ones((N, N), dtype=jnp.float32))
        gate_logit = jnp.zeros((), jnp.float32)
        log_sigma = jnp.zeros((), jnp.float32)
        return {'h': h, 'causal_mask': causal_mask, 'W_lang': W_lang, 'W_grav': W_grav, 'W_V': W_V, 'W_O': W_O, 'gate_logit': gate_logit, 'log_sigma': log_sigma}
    _L1_gnn_all = _L1_gnn_setup()
    _L1_gnn_in = {k: v for k, v in _L1_gnn_all.items() if k in ('W_lang', 'W_grav', 'W_V', 'W_O', 'gate_logit', 'log_sigma')}
    del _L1_gnn_all

    def _L2_gnn_setup():
        import jax, jax.numpy as jnp
        import numpy as np
        DIM = 199
        K_HOP = 3

        def _khop_support(n, k):
            A = np.eye(n, dtype=np.float64)
            idx = np.arange(n)
            A[idx, (idx + 1) % n] = 1.0
            A[(idx + 1) % n, idx] = 1.0
            S = np.linalg.matrix_power(A, k)
            return (S > 0).astype(np.float32)
        key = jax.random.key(seed)
        kx, kk = jax.random.split(key)
        batch, n, f = (128, DIM, 512)
        x = jax.random.normal(kx, (batch, n, f), dtype=jnp.float32)
        support = jnp.asarray(_khop_support(n, K_HOP))
        limit = float(np.sqrt(6.0 / (n + n)))
        kernel = jax.random.uniform(kk, (n, n), minval=-limit, maxval=limit, dtype=jnp.float32)
        bias = jnp.zeros((f,), dtype=jnp.float32)
        return {'x': x, 'support': support, 'kernel': kernel, 'bias': bias}
    _L2_gnn_all = _L2_gnn_setup()
    _L2_gnn_in = {k: v for k, v in _L2_gnn_all.items() if k in ('bias',)}
    del _L2_gnn_all

    def _L3_gnn_setup():
        import jax, jax.numpy as jnp
        import numpy as np
        NEG_SLOPE = 0.01
        key = jax.random.key(seed)
        k1, k2, k3, k4, k5 = jax.random.split(key, 5)
        B, C, N, O = (32, 256, 512, 256)
        x = jax.random.normal(k1, (B, C, N), dtype=jnp.float32)
        wq = jax.random.normal(k2, (C,), dtype=jnp.float32) * (1.0 / np.sqrt(C))
        wk = jax.random.normal(k3, (C,), dtype=jnp.float32) * (1.0 / np.sqrt(C))
        wm = jax.random.normal(k4, (O, C), dtype=jnp.float32) * (1.0 / np.sqrt(C))
        bm = jax.random.normal(k5, (O,), dtype=jnp.float32) * 0.01
        return {'x': x, 'wq': wq, 'wk': wk, 'wm': wm, 'bm': bm}
    _L3_gnn_all = _L3_gnn_setup()
    _L3_gnn_in = {k: v for k, v in _L3_gnn_all.items() if k in ('wq', 'wk', 'bm')}
    del _L3_gnn_all
    return {'x': x, 'adj': adj, 'L0_gnn_wq': _L0_gnn_in['wq'], 'L0_gnn_wk': _L0_gnn_in['wk'], 'L0_gnn_bm': _L0_gnn_in['bm'], 'L1_gnn_W_lang': _L1_gnn_in['W_lang'], 'L1_gnn_W_grav': _L1_gnn_in['W_grav'], 'L1_gnn_W_V': _L1_gnn_in['W_V'], 'L1_gnn_W_O': _L1_gnn_in['W_O'], 'L1_gnn_gate_logit': _L1_gnn_in['gate_logit'], 'L1_gnn_log_sigma': _L1_gnn_in['log_sigma'], 'L2_gnn_bias': _L2_gnn_in['bias'], 'L3_gnn_wq': _L3_gnn_in['wq'], 'L3_gnn_wk': _L3_gnn_in['wk'], 'L3_gnn_bm': _L3_gnn_in['bm']}

def reference(x, adj, L0_gnn_wq, L0_gnn_wk, L0_gnn_bm, L1_gnn_W_lang, L1_gnn_W_grav, L1_gnn_W_V, L1_gnn_W_O, L1_gnn_gate_logit, L1_gnn_log_sigma, L2_gnn_bias, L3_gnn_wq, L3_gnn_wk, L3_gnn_bm):
    import jax
    import jax.numpy as jnp

    def _L0_gnn_ref(x, wq, wk, wm, bm):
        import jax, jax.numpy as jnp
        import numpy as np
        NEG_SLOPE = 0.01
        q = jnp.einsum('c,bcn->bn', wq, x)
        k = jnp.einsum('c,bcn->bn', wk, x)
        scores = q[:, None, :] + k[:, :, None]
        scores = jnp.where(scores > 0, scores, NEG_SLOPE * scores)
        att = jax.nn.softmax(scores, axis=-1)
        agg = jnp.einsum('bcn,bmn->bcm', x, att)
        out = jnp.einsum('oc,bcm->bom', wm, agg) + bm[None, :, None]
        return jax.nn.relu(out)

    def _L1_gnn_ref(h, causal_mask, W_lang, W_grav, W_V, W_O, gate_logit, log_sigma):
        import jax, jax.numpy as jnp
        import numpy as np
        EPS = 1e-08

        def _row_stochastic_causal(A, causal_mask):
            A = A * causal_mask
            deg = jnp.maximum(A.sum(axis=-1, keepdims=True), EPS)
            return A / deg
        z_l = jnp.einsum('bnd,ed->bne', h, W_lang)
        z_g = jnp.einsum('bnd,ed->bne', h, W_grav)
        v = jnp.einsum('bnd,ed->bne', h, W_V)
        N = h.shape[-2]
        not_eye = 1.0 - jnp.eye(N, dtype=h.dtype)
        zn = z_l / jnp.maximum(jnp.linalg.norm(z_l, axis=-1, keepdims=True), EPS)
        A_l = jnp.maximum(jnp.einsum('bnd,bmd->bnm', zn, zn), 0.0) * not_eye
        sq = jnp.sum(z_g * z_g, axis=-1, keepdims=True)
        d2 = jnp.maximum(sq + jnp.swapaxes(sq, -1, -2) - 2.0 * jnp.einsum('bnd,bmd->bnm', z_g, z_g), 0.0)
        sigma = jnp.exp(log_sigma)
        A_g = jnp.exp(-d2 / (2.0 * sigma * sigma)) * not_eye
        K_l = _row_stochastic_causal(A_l, causal_mask)
        K_g = _row_stochastic_causal(A_g, causal_mask)
        w_l = jax.nn.sigmoid(gate_logit)
        K = w_l * K_l + (1.0 - w_l) * K_g
        out = jnp.einsum('bnm,bmd->bnd', K, v)
        return jnp.einsum('bnd,ed->bne', out, W_O)

    def _L2_gnn_ref(x, support, kernel, bias):
        import jax, jax.numpy as jnp
        import numpy as np
        DIM = 199
        K_HOP = 3

        def _khop_support(n, k):
            A = np.eye(n, dtype=np.float64)
            idx = np.arange(n)
            A[idx, (idx + 1) % n] = 1.0
            A[(idx + 1) % n, idx] = 1.0
            S = np.linalg.matrix_power(A, k)
            return (S > 0).astype(np.float32)
        W = support * kernel
        out = jnp.einsum('bnf,nm->bmf', x, W)
        out = out + bias
        return out

    def _L3_gnn_ref(x, wq, wk, wm, bm):
        import jax, jax.numpy as jnp
        import numpy as np
        NEG_SLOPE = 0.01
        q = jnp.einsum('c,bcn->bn', wq, x)
        k = jnp.einsum('c,bcn->bn', wk, x)
        scores = q[:, None, :] + k[:, :, None]
        scores = jnp.where(scores > 0, scores, NEG_SLOPE * scores)
        att = jax.nn.softmax(scores, axis=-1)
        agg = jnp.einsum('bcn,bmn->bcm', x, att)
        out = jnp.einsum('oc,bcm->bom', wm, agg) + bm[None, :, None]
        return jax.nn.relu(out)
    h = jnp.maximum(_layernorm(x, axis=-1), 0.0)
    x = x + _L0_gnn_ref(h, L0_gnn_wq, L0_gnn_wk, adj, L0_gnn_bm)
    h = jnp.maximum(_layernorm(x, axis=-1), 0.0)
    x = x + _L1_gnn_ref(h, adj, L1_gnn_W_lang, L1_gnn_W_grav, L1_gnn_W_V, L1_gnn_W_O, L1_gnn_gate_logit, L1_gnn_log_sigma)
    h = jnp.maximum(_layernorm(x, axis=-1), 0.0)
    x = x + _L2_gnn_ref(h, adj, adj, L2_gnn_bias)
    h = jnp.maximum(_layernorm(x, axis=-1), 0.0)
    x = x + _L3_gnn_ref(h, L3_gnn_wq, L3_gnn_wk, adj, L3_gnn_bm)
    return x

_drawn_inputs = setup_inputs


def setup_inputs(seed=0):
    import zlib

    import numpy as np

    out = dict(_drawn_inputs(seed))
    spreads = {'L2_gnn_bias': (0.0, 0.1)}
    factors = {'L0_gnn_wq': 8.0,
     'L0_gnn_wk': 8.0,
     'L0_gnn_bm': 8.0,
     'L1_gnn_W_lang': 7.162,
     'L3_gnn_wq': 8.0,
     'L3_gnn_wk': 8.0,
     'L3_gnn_bm': 8.0}
    for name, (base, spread) in spreads.items():
        noise = np.random.default_rng([zlib.crc32(name.encode()), seed]).standard_normal(out[name].shape)
        drawn = base * np.exp(spread * noise) if base else spread * noise
        out[name] = jnp.asarray(drawn.astype(out[name].dtype))
    for name, factor in factors.items():
        out[name] = (out[name] * factor).astype(out[name].dtype)
    return out
```

```python
from contextlib import ExitStack

import concourse.bass as bass
from concourse import mybir

F32 = mybir.dt.float32
F32R = mybir.dt.float32r
ALU = mybir.AluOpType
ACT = mybir.ActivationFunctionType
AX = mybir.AxisListType

P = 128
LN_EPS = 1e-5
NORM_EPS = 1e-8
SLOPE = 0.01
FIRST_LOOPED = 4
SMALL_LOADS = 10


def emit(nc, x, adj, wq0, wk0, bm0, w_lang, w_grav, w_v, w_o, gate, log_sigma, bias2, wq3, wk3, bm3, out):
    B, C, N = x.shape
    CT = C // P
    NT = N // P
    D = N
    DT = D // P
    YC = C + 2
    assert B % 2 == 0 and B > FIRST_LOOPED and NT == 4 and CT == 2

    x_view = x.rearrange("b (t p) n -> b p t n", p=P)
    out_view = out.rearrange("b (t p) n -> b p t n", p=P)

    ctx = ExitStack()
    with ctx:
        def sb(name, shape, dt=F32):
            return ctx.enter_context(nc.sbuf_tensor(name, shape, dt))

        def ps(name, shape):
            return ctx.enter_context(nc.psum_tensor(name, shape, F32))

        def split(name, shape):
            return sb(name + "_hi", shape, F32R), sb(name + "_lo", shape, F32R)

        ident = sb("ident", [P, P])
        off_diag = sb("off_diag", [P, P])
        ones = sb("ones", [P, P])
        ones_r = sb("ones_r", [P, P], F32R)
        wy = split("wy", [P, CT, YC])
        wk_rep = [split(f"wk_rep{a}", [P, CT, P]) for a in range(2)]
        wqk_col = sb("wqk_col", [P, 2, 2, CT])
        wqk = split("wqk", [P, 2, 2, CT])
        bm_col = sb("bm_col", [P, 2, CT])
        adj_off = sb("adj_off", [P, CT, C])
        w2 = split("w2", [P, CT, C])
        bias_row = sb("bias_row", [P, N])
        lang_t = split("lang_t", [P, DT, D])
        grav_t = split("grav_t", [P, DT, D])
        vo_t = split("vo_t", [P, DT, D])
        scal = sb("scal", [P, 6])
        eps_col = sb("eps_col", [P, CT])
        mhalf_col = sb("mhalf_col", [P, CT])
        inv_var = scal[:, 2:3]
        w_l = scal[:, 5:6]

        x_a = sb("x_a", [P, 2, CT, N])
        x_b = sb("x_b", [P, CT, N])
        norm = sb("norm", [P, CT, N])
        norm_1 = sb("norm_1", [P, CT, N])
        h_a = split("h_a", [P, CT, N])
        h_b = split("h_b", [P, CT, N])
        stats = sb("stats", [P, 4, CT, 6])
        mean_var = sb("mean_var", [P, 4, CT, 2])
        var_eps = sb("var_eps", [P, 4, CT])
        rstd = sb("rstd", [P, 4, CT])
        y = [split(f"y{a}", [P, NT, C]) for a in range(2)]
        q_col = sb("q_col", [P, 2, NT])
        q_max1 = sb("q_max1", [P, 2])
        q_max = sb("q_max", [P, 2])
        q_sub = sb("q_sub", [P, 2, NT])
        exp_q = sb("exp_q", [P, 2, NT])
        exp_sq = sb("exp_sq", [P, 2, NT])
        u_row = sb("u_row", [P, N])
        v_row = sb("v_row", [P, N])
        e_full = sb("e_full", [P, NT, N])
        e_hl = [split(f"e{a}", [P, NT, N]) for a in range(2)]
        rec = sb("rec", [P, N])
        o_buf = sb("o_buf", [P, 2, CT, N])
        h_t = split("h_t", [P, DT, C])
        z_l = split("z_l", [P, DT, C])
        z_g = split("z_g", [P, DT, C])
        pv = [t[:, :, :].rearrange("p (n q) c -> p n (q c)", n=CT) for t in z_l]
        k_t = [t[:, 0:CT, :] for t in z_g]
        diag_l = sb("diag_l", [P, CT, P])
        diag_g = sb("diag_g", [P, CT, P])
        diag_n = sb("diag_n", [P, CT, P])
        norm2 = sb("norm2", [P, CT])
        inv_norm = sb("inv_norm", [P, CT])
        half_sq = sb("half_sq", [P, CT])
        adj_scaled = sb("adj_scaled", [P, CT, C])
        mix_l = sb("mix_l", [P, CT, C])
        mix_g = sb("mix_g", [P, CT, C])
        degree = sb("degree", [P, 2 * CT])
        degree_inv = sb("degree_inv", [P, 2 * CT])
        coef = sb("coef", [P, 2 * CT])
        weight = sb("weight", [P, 2 * CT])
        room = [x_a[:, :, :, :].rearrange("p a t n -> p (a t) n"), o_buf[:, :, :, :].rearrange("p a t n -> p (a t) n")]
        adj_in = norm[:, 0, :].rearrange("p (t c) -> p t c", t=CT)
        w_o_t = e_full
        w2_full = mix_l

        ps_a = ps("ps_a", [P, 2, 512])
        ps_b = ps("ps_b", [P, 2, 512])
        ps_c = ps("ps_c", [P, 2, 512])
        ps_6 = ps("ps_6", [P, 512])
        ps_7 = ps("ps_7", [P, 512])
        ps_y = [(ps_a, ps_c), (ps_c, ps_b)]
        ps_row = [ps_7, ps_6]
        ps_o = [ps_c, ps_a]
        ps_zl = ps_c[:, :, :].rearrange("p q (t c) -> p (q t) c", t=2)
        ps_zg = ps_a[:, :, :].rearrange("p q (t c) -> p (q t) c", t=2)
        ps_ht = ps_zl
        gram_l = ps_b[:, 0, :].rearrange("p (t c) -> p t c", t=CT)
        gram_g = ps_b[:, 1, :].rearrange("p (t c) -> p t c", t=CT)
        ps_kt = ps_6[:, :].rearrange("p (t c) -> p t c", t=CT)
        ps_setup = [ps_a, ps_b, ps_c]

        def diagonal_blocks(bank):
            return bank.rearrange("p (u w) -> p u w", w=P)[:, 0:4:3, :]

        def one(name):
            return ctx.enter_context(nc.semaphore(name))

        def by_attention(name):
            return [one(f"{name}_{a}") for a in range(2)]

        def by_layer(name):
            return [one(f"{name}_{layer}") for layer in range(4)]

        setup_const = one("setup_const")
        setup_ident = one("setup_ident")
        setup_pe = one("setup_pe")
        setup_hi = one("setup_hi")
        setup_lo = one("setup_lo")
        setup_dve = one("setup_dve")
        setup_scal = one("setup_scal")
        stored = one("stored")
        pv_done = one("pv_done")
        gram_done = one("gram_done")
        sq_added = one("sq_added")
        norms_spread = one("norms_spread")
        kt_done = one("kt_done")
        kp_done = one("kp_done")
        ht_done = one("ht_done")
        zl_done = one("zl_done")
        zg_done = one("zg_done")
        l2_done = one("l2_done")
        diags = one("diags")
        norms2 = one("norms2")
        norm_clamped = one("norm_clamped")
        norm_inv = one("norm_inv")
        norm_diag = one("norm_diag")
        grav_arg = one("grav_arg")
        grav_exp = one("grav_exp")
        adj_scale = one("adj_scale")
        mixed_l = one("mixed_l")
        mixed_g = one("mixed_g")
        degrees = one("degrees")
        deg_max = one("deg_max")
        deg_inv = one("deg_inv")
        weighted = one("weighted")
        coefs = one("coefs")
        grav_part = one("grav_part")
        k_done = one("k_done")
        kt_hi = one("kt_hi")
        kt_lo = one("kt_lo")
        pv_hi = one("pv_hi")
        pv_lo = one("pv_lo")
        ht_hi = one("ht_hi")
        ht_lo = one("ht_lo")
        zl_hi = one("zl_hi")
        zl_lo = one("zl_lo")
        zg_hi = one("zg_hi")
        zg_lo = one("zg_lo")
        x1_done = one("x1_done")
        x2_done = one("x2_done")
        x_bias = one("x_bias")
        x3_done = one("x3_done")
        x4_done = one("x4_done")
        dve_go = one("dve_go")
        pool_go = one("pool_go")
        y_done = by_attention("y_done")
        keys_done = by_attention("keys_done")
        sums_done = by_attention("sums_done")
        o_done = by_attention("o_done")
        q_read = by_attention("q_read")
        q_maxed = by_attention("q_maxed")
        q_all = by_attention("q_all")
        q_subbed = by_attention("q_subbed")
        exp_q_done = by_attention("exp_q_done")
        y_hi = by_attention("y_hi")
        y_lo = by_attention("y_lo")
        row_clamped = by_attention("row_clamped")
        row_exped = by_attention("row_exped")
        e_v = by_attention("e_v")
        e_01 = by_attention("e_01")
        e_23 = by_attention("e_23")
        e_hi_01 = by_attention("e_hi_01")
        e_hi_23 = by_attention("e_hi_23")
        e_lo_01 = by_attention("e_lo_01")
        e_lo_23 = by_attention("e_lo_23")
        log_sum = by_attention("log_sum")
        rec_done = by_attention("rec_done")
        o_scaled = by_attention("o_scaled")
        o_relu = by_attention("o_relu")
        stats_done = by_layer("stats_done")
        mean_var_done = by_layer("mean_var_done")
        var_eps_done = by_layer("var_eps_done")
        rstd_done = by_layer("rstd_done")
        norm_done = by_layer("norm_done")
        h_hi = by_layer("h_hi")
        h_lo = by_layer("h_lo")
        loaded = [one(f"loaded_{k}") for k in range(2)]
        setup_load = [one(f"setup_load_{k}") for k in range(3)]

        def steps(eng, body):
            for b in range(-1, FIRST_LOOPED):
                body(b, b % 2, b // 2)
            with eng.Fori(FIRST_LOOPED // 2, B // 2 - 1) as turn:
                body(2 * turn, 0, turn)
                body(2 * turn + 1, 1, turn)
            for b in range(B - 2, B + 2):
                body(b, b % 2, b // 2)

        def exists(e):
            return not isinstance(e, int) or 0 <= e < B

        def later(e):
            return not isinstance(e, int) or e > 0

        block = ctx.enter_context(nc.Block())

        @block.sync
        def _(sp):
            sp.dma_start(adj_in, adj.rearrange("(t p) c -> p t c", p=P)).then_inc(setup_load[0], 16)
            for a, (wq, wk, bm) in enumerate(((wq0, wk0, bm0), (wq3, wk3, bm3))):
                sp.dma_start(wqk_col[:, a, 0, :], wq.rearrange("(t p) -> p t", p=P), allow_slow_non_contiguous=True).then_inc(setup_load[0], 16)
                sp.dma_start(wqk_col[:, a, 1, :], wk.rearrange("(t p) -> p t", p=P), allow_slow_non_contiguous=True).then_inc(setup_load[0], 16)
                sp.dma_start(bm_col[:, a, :], bm.rearrange("(t p) -> p t", p=P), allow_slow_non_contiguous=True).then_inc(setup_load[0], 16)
            sp.dma_start(scal[:, 0:1], gate.partition_broadcast(P)).then_inc(setup_load[0], 16)
            sp.dma_start(scal[:, 1:2], log_sigma.partition_broadcast(P)).then_inc(setup_load[0], 16)
            sp.dma_start(bias_row[:, :], bias2.partition_broadcast(P)).then_inc(setup_load[0], 16)
            for n, w in enumerate((w_lang, w_grav, w_o, w_v)):
                if n >= 2:
                    sp.wait_ge(setup_pe, 1 + 2 * (n - 1))
                sp.dma_start(room[n % 2], w.rearrange("(t p) d -> p t d", p=P)).then_inc(setup_load[1 + n % 2], 16)

            def body(b, k, turn):
                next_k, next_turn = (1, turn) if k == 0 else (0, turn + 1)
                if exists(b + 1):
                    if later(b):
                        sp.wait_ge(x3_done, b)
                    else:
                        sp.wait_ge(setup_pe, 7)
                    sp.dma_start(x_a[:, next_k, :, :], x_view[b + 1]).then_inc(loaded[next_k], 16)
                if exists(b - 2):
                    sp.wait_ge(x4_done, b - 1)
                    sp.dma_start(out_view[b - 2], o_buf[:, 1, :, :]).then_inc(stored, 16)

            steps(sp, body)
            sp.wait_ge(stored, 16 * B)

        @block.tensor
        def _(pe):
            def passes(out, left, right, start, stop):
                nc.tensor.matmul(out, left[0], right[0], start=start, stop=False, skip_group_check=True)
                nc.tensor.matmul(out, left[0], right[1], start=False, stop=False, skip_group_check=True)
                return nc.tensor.matmul(out, left[1], right[0], start=False, stop=stop, skip_group_check=True)

            def transposed(bank_pair, w, half):
                for q in range(2):
                    for t in range(DT):
                        c = (2 * half + q) * P
                        last = nc.tensor.transpose(bank_pair[:, q, t * P:(t + 1) * P], w[:, t, c:c + P], ident[:, :])
                return last

            def setup():
                pe.wait_ge(setup_load[0], SMALL_LOADS * 16)
                pe.wait_ge(setup_ident, 2)
                for t in range(CT):
                    for o in range(CT):
                        last = nc.tensor.transpose(ps_6[:, t * C + o * P:t * C + (o + 1) * P],
                                                   adj_in[:, o, t * P:(t + 1) * P], ident[:, :])
                last.then_inc(setup_pe, 1)
                pe.wait_ge(setup_load[1], 16)
                transposed(ps_a, room[0], 0).then_inc(setup_pe, 1)
                transposed(ps_b, room[0], 1).then_inc(setup_pe, 1)
                pe.wait_ge(setup_load[2], 16)
                transposed(ps_c, room[1], 0).then_inc(setup_pe, 1)
                pe.wait_ge(setup_lo, 2)
                transposed(ps_a, room[1], 1).then_inc(setup_pe, 1)
                pe.wait_ge(setup_load[1], 32)
                pe.wait_ge(setup_lo, 3)
                transposed(ps_b, room[0], 0).then_inc(setup_pe, 1)
                pe.wait_ge(setup_lo, 4)
                transposed(ps_c, room[0], 1).then_inc(setup_pe, 1)
                pe.wait_ge(setup_load[2], 32)
                pe.wait_ge(setup_hi, 7)
                pe.wait_ge(setup_lo, 5)
                for half, pair in ((0, ps_a), (1, ps_b)):
                    for q in range(2):
                        c = (2 * half + q) * P
                        for t in range(DT):
                            last = nc.tensor.matmul(pair[:, q, :], room[1][:, t, c:c + P], w_o_t[:, t, :],
                                                    start=(t == 0), stop=(t == DT - 1))
                    last.then_inc(setup_pe, 1)

            def project(a, e):
                h = (h_a, h_b)[a]
                pe.wait_ge(h_lo[(0, 3)[a]], e + 1)
                if a == 0 and later(e):
                    pe.wait_ge(zg_lo, e)
                if a == 0 and later(e - 1):
                    pe.wait_ge(y_lo[1], e - 1)
                if a == 1:
                    pe.wait_ge(x3_done, e + 1)
                for n in range(NT):
                    if a == 1 and n == 0 and exists(e + 1):
                        pe.wait_ge(zl_lo, e + 2)
                    for t in range(CT):
                        last = passes(ps_y[a][n // 2][:, n % 2, 0:YC],
                                      [x[:, t, n * P:(n + 1) * P] for x in h], [w[:, t, :] for w in wy],
                                      t == 0, t == CT - 1)
                last.then_inc(y_done[a], 1)
                if a == 0 and later(e):
                    pe.wait_ge(log_sum[0], e)
                if a == 1 and later(e):
                    pe.wait_ge(log_sum[1], e)
                for t in range(CT):
                    last = passes(ps_row[a][:, :], [w[:, t, :] for w in wk_rep[a]], [x[:, t, :] for x in h],
                                  t == 0, t == CT - 1)
                last.then_inc(keys_done[a], 1)

            def attend(a, e):
                pe.wait_ge(e_lo_01[a], e + 1)
                pe.wait_ge(e_lo_23[a], e + 1)
                pe.wait_ge(y_lo[a], e + 1)
                if a == 1 and exists(e + 1):
                    pe.wait_ge(pv_lo, e + 2)
                for n in range(NT):
                    for half in range(2):
                        last = nc.tensor.matmul(ps_row[a][:, :], ones_r[:, :], e_hl[a][half][:, n, :],
                                                start=(n == 0 and half == 0), stop=(n == NT - 1 and half == 1))
                last.then_inc(sums_done[a], 1)
                for o in range(CT):
                    for n in range(NT):
                        last = passes(ps_o[a][:, o, :], [v[:, n, o * P:(o + 1) * P] for v in y[a]],
                                      [v[:, n, :] for v in e_hl[a]], n == 0, n == NT - 1)
                last.then_inc(o_done[a], 1)

            def grams(e):
                pe.wait_ge(zg_lo, e + 1)
                if later(e):
                    pe.wait_ge(y_lo[1], e)
                for gram, z in ((gram_l, z_l), (gram_g, z_g)):
                    for n in range(CT):
                        for t in range(DT):
                            last = passes(gram[:, n, :], [v[:, t, n * P:(n + 1) * P] for v in z],
                                          [v[:, t, :] for v in z], n == 0 and t == 0, t == DT - 1)
                last.then_inc(gram_done, 1)

            def gram_rows(e):
                pe.wait_ge(diags, e + 1)
                for n in range(CT):
                    last = nc.tensor.matmul(gram_g[:, n, :], ones[:, :], diag_g[:, :, :].rearrange("p t c -> p (t c)"),
                                            start=False, stop=True, skip_group_check=True)
                last.then_inc(sq_added, 1)
                pe.wait_ge(norm_diag, e + 1)
                if later(e):
                    pe.wait_ge(row_clamped[1], e)
                nc.tensor.matmul(ps_6[:, 0:C], ones[:, :], diag_n[:, :, :].rearrange("p t c -> p (t c)"),
                                 start=True, stop=True).then_inc(norms_spread, 1)

            def values(e):
                if exists(e + 1):
                    pe.wait_ge(y_lo[0], e + 2)
                for n in range(CT):
                    for t in range(DT):
                        last = passes(ps_a[:, n, :], [v[:, t, n * P:(n + 1) * P] for v in h_t],
                                      [w[:, t, :] for w in vo_t], t == 0, t == DT - 1)
                last.then_inc(pv_done, 1)

            def mix(e):
                pe.wait_ge(k_done, e + 1)
                for t in range(CT):
                    for n in range(CT):
                        last = nc.tensor.transpose(ps_kt[:, t, n * P:(n + 1) * P], mix_l[:, n, t * P:(t + 1) * P],
                                                   ident[:, :])
                last.then_inc(kt_done, 1)
                pe.wait_ge(kt_lo, e + 1)
                pe.wait_ge(pv_lo, e + 1)
                for n in range(CT):
                    for t in range(CT):
                        last = passes(ps_b[:, n, :], [v[:, t, n * P:(n + 1) * P] for v in k_t],
                                      [v[:, t, :] for v in pv], t == 0, t == CT - 1)
                last.then_inc(kp_done, 1)

            def turn_h(e):
                pe.wait_ge(norm_done[1], e + 1)
                for t in range(DT):
                    for n in range(CT):
                        last = nc.tensor.transpose(ps_ht[:, t, n * P:(n + 1) * P], norm_1[:, n, t * P:(t + 1) * P],
                                                   ident[:, :])
                last.then_inc(ht_done, 1)

            def fixed(e):
                pe.wait_ge(h_lo[2], e + 1)
                for m in range(CT):
                    for n in range(CT):
                        last = passes(ps_b[:, m, :], [w[:, n, m * P:(m + 1) * P] for w in w2],
                                      [v[:, n, :] for v in h_a], n == 0, n == CT - 1)
                last.then_inc(l2_done, 1)

            def z_of(target, weight_t, done):
                for o in range(DT):
                    for t in range(DT):
                        last = passes(target[:, o, :], [w[:, t, o * P:(o + 1) * P] for w in weight_t],
                                      [v[:, t, :] for v in h_t], o % 2 == 0 and t == 0, t == DT - 1)
                last.then_inc(done, 1)

            def body(b, k, turn):
                if exists(b):
                    project(0, b)
                if exists(b - 1):
                    grams(b - 1)
                    values(b - 1)
                    gram_rows(b - 1)
                if exists(b):
                    attend(0, b)
                if exists(b - 1):
                    mix(b - 1)
                if exists(b - 2):
                    attend(1, b - 2)
                if exists(b):
                    turn_h(b)
                if exists(b - 1):
                    fixed(b - 1)
                if exists(b):
                    pe.wait_ge(ht_lo, b + 1)
                    z_of(ps_zl, lang_t, zl_done)
                    if later(b - 1):
                        pe.wait_ge(o_scaled[1], b - 1)
                    z_of(ps_zg, grav_t, zg_done)
                if exists(b - 1):
                    project(1, b - 1)

            setup()
            steps(pe, body)

        @block.scalar
        def _(act):
            def setup():
                nc.scalar.preload_act_table_set("natural_log_exp_and_others")
                act.wait_ge(setup_load[0], SMALL_LOADS * 16)
                nc.scalar.activation(scal[:, 2:3], scal[:, 1:2], ACT.Exp, scale=-2.0)
                nc.scalar.activation(scal[:, 3:4], scal[:, 0:1], ACT.Exp, scale=-1.0)
                nc.scalar.copy(wqk[0][:, :, :, :], wqk_col[:, :, :, :]).then_inc(setup_scal, 1)
                act.wait_ge(setup_pe, 1)
                nc.scalar.copy(wy[0][:, :, 0:C], ps_6[:, :].rearrange("p (t c) -> p t c", t=CT)).then_inc(setup_hi, 1)
                for n in range(8):
                    act.wait_ge(setup_pe, n + 2)
                    rows = slice(2 * (n % 2), 2 * (n % 2) + 2)
                    target = (lang_t[0], grav_t[0], w_o_t, vo_t[0])[n // 2]
                    source = (ps_a, ps_b, ps_c, ps_a, ps_b, ps_c, ps_a, ps_b)[n]
                    nc.scalar.copy(target[:, rows, :], source[:, :, :]).then_inc(setup_hi, 1)

            def projected(a, e):
                act.wait_ge(q_read[a], e + 1)
                if later(e):
                    act.wait_ge(o_done[a], e)
                for g in range(2):
                    last = nc.scalar.copy(y[a][0][:, 2 * g:2 * g + 2, :], ps_y[a][g][:, :, 0:C])
                last.then_inc(y_hi[a], 1)
                act.wait_ge(q_subbed[a], e + 1)
                if later(e):
                    act.wait_ge(e_23[a], e)
                nc.scalar.activation(exp_q[:, a, :], q_sub[:, a, :], ACT.Exp)
                nc.scalar.activation(exp_sq[:, a, :], q_sub[:, a, :], ACT.Exp, scale=SLOPE).then_inc(exp_q_done[a], 1)
                act.wait_ge(row_clamped[a], e + 1)
                nc.scalar.activation(v_row[:, :], v_row[:, :], ACT.Exp, scale=SLOPE - 1.0)
                nc.scalar.activation(u_row[:, :], u_row[:, :], ACT.Exp, scale=1.0 - SLOPE).then_inc(row_exped[a], 1)

            def e_high(a, e):
                act.wait_ge(e_01[a], e + 1)
                nc.scalar.copy(e_hl[a][0][:, 0:2, :], e_full[:, 0:2, :]).then_inc(e_hi_01[a], 1)
                act.wait_ge(e_23[a], e + 1)
                nc.scalar.copy(e_hl[a][0][:, 2:4, :], e_full[:, 2:4, :]).then_inc(e_hi_23[a], 1)

            def inverse_sums(a, e):
                act.wait_ge(sums_done[a], e + 1)
                if a == 0 and later(e - 2):
                    act.wait_ge(o_scaled[1], e - 2)
                elif a == 0 and later(e):
                    act.wait_ge(o_scaled[0], e)
                if a == 1 and exists(e + 2):
                    act.wait_ge(o_scaled[0], e + 3)
                elif a == 1 and later(e):
                    act.wait_ge(o_scaled[1], e)
                nc.scalar.activation(rec[:, :], ps_row[a][:, :], ACT.Ln).then_inc(log_sum[a], 1)
                act.wait_ge(log_sum[a], e + 1)
                nc.scalar.activation(rec[:, :], rec[:, :], ACT.Exp, scale=-1.0).then_inc(rec_done[a], 1)

            def biased_relu(a, e):
                act.wait_ge(o_scaled[a], e + 1)
                for o in range(CT):
                    last = nc.scalar.activation(o_buf[:, a, o, :], o_buf[:, a, o, :], ACT.Relu,
                                                bias=bm_col[:, a, o:o + 1])
                last.then_inc(o_relu[a], 1)

            def h_high(layer, e):
                act.wait_ge(norm_done[layer], e + 1)
                if layer == 0 and later(e):
                    act.wait_ge(keys_done[0], e)
                if layer == 0 and later(e - 1):
                    act.wait_ge(l2_done, e - 1)
                if layer == 2 and exists(e + 1):
                    act.wait_ge(keys_done[0], e + 2)
                if layer == 3 and later(e):
                    act.wait_ge(keys_done[1], e)
                h = h_b if layer == 3 else h_a
                nc.scalar.activation(h[0][:, :, :], norm[:, :, :], ACT.Relu).then_inc(h_hi[layer], 1)

            def body(b, k, turn):
                if exists(b - 2):
                    projected(1, b - 2)
                    e_high(1, b - 2)
                if exists(b):
                    projected(0, b)
                    e_high(0, b)
                if exists(b - 1):
                    act.wait_ge(pv_done, b)
                    nc.scalar.copy(pv[0], ps_a[:, :, :]).then_inc(pv_hi, 1)
                    act.wait_ge(grav_arg, b)
                    nc.scalar.activation(mix_g[:, :, :], mix_g[:, :, :], ACT.Exp, scale=inv_var).then_inc(grav_exp, 1)
                if exists(b):
                    inverse_sums(0, b)
                if exists(b - 1):
                    act.wait_ge(kt_done, b)
                    nc.scalar.copy(k_t[0], ps_kt).then_inc(kt_hi, 1)
                if exists(b):
                    biased_relu(0, b)
                if exists(b - 1):
                    h_high(2, b - 1)
                if exists(b - 2):
                    inverse_sums(1, b - 2)
                    biased_relu(1, b - 2)
                if exists(b):
                    act.wait_ge(ht_done, b + 1)
                    if later(b):
                        act.wait_ge(pv_done, b)
                    nc.scalar.activation(h_t[0][:, :, :], ps_ht, ACT.Relu).then_inc(ht_hi, 1)
                if exists(b):
                    act.wait_ge(zl_done, b + 1)
                    if later(b):
                        act.wait_ge(kp_done, b)
                    nc.scalar.copy(z_l[0][:, :, :], ps_zl).then_inc(zl_hi, 1)
                if exists(b - 1):
                    h_high(3, b - 1)
                if exists(b):
                    act.wait_ge(zg_done, b + 1)
                    nc.scalar.copy(z_g[0][:, :, :], ps_zg).then_inc(zg_hi, 1)
                if exists(b + 1):
                    h_high(0, b + 1)

            setup()
            steps(act, body)

        @block.vector
        def _(dve):
            def low(out_lo, full, hi):
                return nc.vector.tensor_tensor(out_lo, full, hi.bitcast(F32), ALU.subtract)

            def setup():
                nc.vector.memset(eps_col[:, :], LN_EPS)
                nc.vector.memset(mhalf_col[:, :], -0.5)
                nc.vector.memset(ones[:, :], 1.0).then_inc(setup_dve, 1)
                dve.wait_ge(setup_dve, 1)
                nc.vector.tensor_copy(ones_r[:, :], ones[:, :]).then_inc(setup_const, 1)
                dve.wait_ge(setup_ident, 2)
                nc.vector.tensor_scalar(off_diag[:, :], ident[:, :], -1.0, 1.0, ALU.mult, ALU.add)
                dve.wait_ge(setup_scal, 1)
                low(wqk[1][:, :, :, :], wqk_col[:, :, :, :], wqk[0][:, :, :, :])
                nc.vector.tensor_scalar_add(scal[:, 4:5], scal[:, 3:4], 1.0).then_inc(setup_dve, 1)
                dve.wait_ge(setup_dve, 2)
                nc.vector.reciprocal(scal[:, 5:6], scal[:, 4:5])
                for a in range(2):
                    for half in range(2):
                        part = wqk[half][:, a, :, :].bitcast(F32)
                        for t in range(CT):
                            nc.vector.tensor_copy(wk_rep[a][half][:, t, :], part[:, 1, t:t + 1].to_broadcast([P, P]))
                            nc.vector.tensor_copy(wy[half][:, t, C + a:C + a + 1], part[:, 0, t:t + 1])
                nc.vector.tensor_tensor(w2_full[:, :, :], adj_in, adj_in, ALU.mult)
                for t in range(CT):
                    for c in range(CT):
                        block_of = lambda m: m[:, t, c * P:(c + 1) * P]
                        if t == c:
                            last = nc.vector.tensor_tensor(block_of(adj_off), block_of(adj_in), off_diag[:, :], ALU.mult)
                        else:
                            last = nc.vector.tensor_copy(block_of(adj_off), block_of(adj_in))
                last.then_inc(setup_dve, 1)
                dve.wait_ge(setup_dve, 3)
                nc.vector.tensor_scalar(weight[:, CT:2 * CT], w_l.to_broadcast([P, CT]), -1.0, 1.0, ALU.mult, ALU.add)
                nc.vector.tensor_copy(w2[0][:, :, :], w2_full[:, :, :]).then_inc(setup_dve, 1)
                dve.wait_ge(setup_dve, 4)
                low(w2[1][:, :, :], w2_full[:, :, :], w2[0][:, :, :])
                dve.wait_ge(setup_hi, 1)
                low(wy[1][:, :, 0:C], ps_6[:, :].rearrange("p (t c) -> p t c", t=CT), wy[0][:, :, 0:C]).then_inc(setup_lo, 1)
                for n in (0, 1, 2, 3, 6, 7):
                    dve.wait_ge(setup_hi, n + 2)
                    rows = slice(2 * (n % 2), 2 * (n % 2) + 2)
                    target = (lang_t, grav_t, None, vo_t)[n // 2]
                    source = (ps_a, ps_b, ps_c, ps_a, ps_b, ps_c, ps_a, ps_b)[n]
                    low(target[1][:, rows, :], source[:, :, :], target[0][:, rows, :]).then_inc(setup_lo, 1)

            def norm_stats(layer, e, x_in):
                for t in range(CT):
                    last = nc.vector.bn_stats(stats[:, layer, t, :], x_in[:, t, :])
                last.then_inc(stats_done[layer], 1)
                dve.wait_ge(stats_done[layer], e + 1)
                if later(e):
                    dve.wait_ge(norm_done[layer], e)
                dve.sem_inc(dve_go, 1)
                for t in range(CT):
                    last = nc.vector.bn_aggr(mean_var[:, layer, t, :], stats[:, layer, t, :])
                last.then_inc(mean_var_done[layer], 1)

            def normalise(layer, e, x_in):
                dve.wait_ge(rstd_done[layer], e + 1)
                target = norm_1 if layer == 1 else norm
                if layer == 1 and later(e):
                    dve.wait_ge(ht_done, e)
                if layer == 2:
                    if exists(e + 1):
                        dve.wait_ge(h_lo[0], e + 2)
                    elif later(e):
                        dve.wait_ge(h_lo[3], e)
                if layer == 3:
                    dve.wait_ge(h_lo[2], e + 1)
                if layer == 0 and later(e - 1):
                    dve.wait_ge(h_lo[3], e - 1)
                elif layer == 0 and later(e):
                    dve.wait_ge(h_lo[0], e)
                for t in range(CT):
                    last = nc.vector.tensor_scalar(target[:, t, :], x_in[:, t, :], mean_var[:, layer, t, 0:1],
                                                   rstd[:, layer, t:t + 1], ALU.subtract, ALU.mult)
                last.then_inc(norm_done[layer], 1)

            def h_low(layer, e):
                dve.wait_ge(h_hi[layer], e + 1)
                h = h_b if layer == 3 else h_a
                nc.vector.scalar_tensor_tensor(h[1][:, :, :].rearrange("p t n -> p (t n)"),
                                               norm[:, :, :].rearrange("p t n -> p (t n)"), 0.0,
                                               h[0][:, :, :].bitcast(F32).rearrange("p t n -> p (t n)"),
                                               ALU.max, ALU.subtract).then_inc(h_lo[layer], 1)

            def projected(a, e):
                dve.wait_ge(y_done[a], e + 1)
                if later(e):
                    dve.wait_ge(q_subbed[a], e)
                for g in range(2):
                    last = nc.vector.tensor_copy(q_col[:, a, 2 * g:2 * g + 2], ps_y[a][g][:, :, C + a])
                last.then_inc(q_read[a], 1)
                dve.wait_ge(q_read[a], e + 1)
                if later(e):
                    dve.wait_ge(q_all[a], e)
                nc.vector.reduce_max(q_max1[:, a:a + 1], q_col[:, a, :], axis=AX.X).then_inc(q_maxed[a], 1)
                dve.wait_ge(y_hi[a], e + 1)
                for g in range(2):
                    last = low(y[a][1][:, 2 * g:2 * g + 2, :], ps_y[a][g][:, :, 0:C], y[a][0][:, 2 * g:2 * g + 2, :])
                last.then_inc(y_lo[a], 1)
                dve.wait_ge(q_all[a], e + 1)
                if later(e):
                    dve.wait_ge(exp_q_done[a], e)
                nc.vector.tensor_scalar(q_sub[:, a, :], q_col[:, a, :], q_max[:, a:a + 1], None,
                                        ALU.subtract).then_inc(q_subbed[a], 1)
                dve.wait_ge(keys_done[a], e + 1)
                other_rows_used(a, e, e_23)
                nc.vector.tensor_scalar(v_row[:, :], ps_row[a][:, :], q_max[:, a:a + 1], 0.0, ALU.add, ALU.max)
                nc.vector.tensor_scalar(u_row[:, :], ps_row[a][:, :], q_max[:, a:a + 1], 0.0, ALU.add,
                                        ALU.min).then_inc(row_clamped[a], 1)

            def other_rows_used(a, e, step):
                if a == 1 and exists(e + 1):
                    dve.wait_ge(step[0], e + 2)
                elif a == 1 and later(e):
                    dve.wait_ge(step[1], e)
                if a == 0 and later(e - 1):
                    dve.wait_ge(step[1], e - 1)
                elif a == 0 and later(e):
                    dve.wait_ge(step[0], e)

            def exponentials(a, e):
                dve.wait_ge(exp_q_done[a], e + 1)
                dve.wait_ge(row_exped[a], e + 1)
                other_rows_used(a, e, e_lo_01)
                other_rows_used(a, e, e_lo_23)
                for n in range(NT):
                    last = nc.vector.tensor_scalar(e_full[:, n, :], v_row[:, :], exp_sq[:, a, n:n + 1], None, ALU.mult)
                last.then_inc(e_v[a], 1)
                dve.wait_ge(e_v[a], e + 1)
                for n in range(NT):
                    last = nc.vector.scalar_tensor_tensor(e_full[:, n, :], u_row[:, :], exp_q[:, a, n:n + 1],
                                                          e_full[:, n, :], ALU.mult, ALU.max)
                    if n == 1:
                        last.then_inc(e_01[a], 1)
                last.then_inc(e_23[a], 1)
                dve.wait_ge(e_hi_01[a], e + 1)
                low(e_hl[a][1][:, 0:2, :], e_full[:, 0:2, :], e_hl[a][0][:, 0:2, :]).then_inc(e_lo_01[a], 1)

            def gram_diagonals(e):
                dve.wait_ge(gram_done, e + 1)
                if later(e):
                    dve.wait_ge(sq_added, e)
                    dve.wait_ge(norms2, e)
                eye = ident[:, :].unsqueeze(1).to_broadcast([P, CT, P])
                nc.vector.tensor_tensor(diag_l[:, :, :], diagonal_blocks(ps_b[:, 0, :]), eye, ALU.mult)
                nc.vector.scalar_tensor_tensor(diag_g[:, :, :], diagonal_blocks(ps_b[:, 1, :]), -0.5, eye,
                                               ALU.mult, ALU.mult).then_inc(diags, 1)
                dve.wait_ge(diags, e + 1)
                nc.vector.reduce_sum(norm2[:, :], diag_l[:, :, :], axis=AX.X)
                nc.vector.reduce_sum(half_sq[:, :], diag_g[:, :, :], axis=AX.X).then_inc(norms2, 1)
                dve.wait_ge(norms2, e + 1)
                nc.vector.tensor_scalar_max(norm2[:, :], norm2[:, :], NORM_EPS * NORM_EPS).then_inc(norm_clamped, 1)

            def mixing(e):
                dve.wait_ge(norm_inv, e + 1)
                if later(e):
                    dve.wait_ge(norms_spread, e)
                for t in range(CT):
                    last = nc.vector.tensor_scalar(diag_n[:, t, :], ident[:, :], inv_norm[:, t:t + 1], None, ALU.mult)
                last.then_inc(norm_diag, 1)
                if later(e):
                    dve.wait_ge(coefs, e)
                nc.vector.tensor_scalar(weight[:, 0:CT], inv_norm[:, :], w_l, None, ALU.mult).then_inc(weighted, 1)
                dve.wait_ge(sq_added, e + 1)
                if later(e):
                    dve.wait_ge(k_done, e)
                for n in range(CT):
                    last = nc.vector.tensor_scalar(mix_g[:, n, :], gram_g[:, n, :], half_sq[:, n:n + 1], 0.0,
                                                   ALU.add, ALU.min)
                last.then_inc(grav_arg, 1)
                dve.wait_ge(norms_spread, e + 1)
                if later(e):
                    dve.wait_ge(mixed_l, e)
                nc.vector.tensor_tensor(adj_scaled[:, :, :], adj_off[:, :, :],
                                        ps_6[:, 0:C].unsqueeze(1).to_broadcast([P, CT, C]), ALU.mult).then_inc(adj_scale, 1)
                dve.wait_ge(adj_scale, e + 1)
                if later(e):
                    dve.wait_ge(kt_done, e)
                    dve.wait_ge(deg_inv, e)
                for n in range(CT):
                    last = nc.vector.scalar_tensor_tensor(mix_l[:, n, :], gram_l[:, n, :], 0.0, adj_scaled[:, n, :],
                                                          ALU.max, ALU.mult, accum_out=degree[:, n:n + 1])
                last.then_inc(mixed_l, 1)
                dve.wait_ge(grav_exp, e + 1)
                for n in range(CT):
                    last = nc.vector.scalar_tensor_tensor(mix_g[:, n, :], mix_g[:, n, :], 1.0, adj_off[:, n, :],
                                                          ALU.mult, ALU.mult, accum_out=degree[:, CT + n:CT + n + 1])
                last.then_inc(mixed_g, 1)
                dve.wait_ge(mixed_g, e + 1)
                nc.vector.tensor_tensor(degree[:, 0:CT], degree[:, 0:CT], inv_norm[:, :], ALU.mult).then_inc(degrees, 1)
                dve.wait_ge(degrees, e + 1)
                nc.vector.tensor_scalar_max(degree[:, :], degree[:, :], NORM_EPS).then_inc(deg_max, 1)
                dve.wait_ge(deg_max, e + 1)
                nc.vector.reciprocal(degree_inv[:, :], degree[:, :]).then_inc(deg_inv, 1)
                dve.wait_ge(deg_inv, e + 1)
                nc.vector.tensor_tensor(coef[:, :], degree_inv[:, :], weight[:, :], ALU.mult).then_inc(coefs, 1)
                dve.wait_ge(coefs, e + 1)
                for n in range(CT):
                    last = nc.vector.tensor_scalar(mix_g[:, n, :], mix_g[:, n, :], coef[:, CT + n:CT + n + 1], None, ALU.mult)
                last.then_inc(grav_part, 1)
                dve.wait_ge(grav_part, e + 1)
                for n in range(CT):
                    last = nc.vector.scalar_tensor_tensor(mix_l[:, n, :], mix_l[:, n, :], coef[:, n:n + 1],
                                                          mix_g[:, n, :], ALU.mult, ALU.add)
                last.then_inc(k_done, 1)

            def scale_out(a, e):
                dve.wait_ge(rec_done[a], e + 1)
                dve.wait_ge(o_done[a], e + 1)
                if a == 0 and later(e):
                    dve.wait_ge(x1_done, e)
                if a == 1 and later(e):
                    dve.wait_ge(stored, 16 * e)
                nc.vector.tensor_tensor(o_buf[:, a, :, :], ps_o[a][:, :, :],
                                        rec[:, :].unsqueeze(1).to_broadcast([P, CT, N]), ALU.mult).then_inc(o_scaled[a], 1)

            def body(b, k, turn):
                x_now, x_last, x_next = x_a[:, k, :, :], x_a[:, 1 - k, :, :], x_a[:, 1 - k, :, :]
                if exists(b - 2):
                    projected(1, b - 2)
                    exponentials(1, b - 2)
                if exists(b):
                    projected(0, b)
                    exponentials(0, b)
                if exists(b - 1):
                    gram_diagonals(b - 1)
                    dve.wait_ge(pv_hi, b)
                    low(pv[1], ps_a[:, :, :], pv[0]).then_inc(pv_lo, 1)
                    mixing(b - 1)
                    dve.wait_ge(kt_hi, b)
                    low(k_t[1], ps_kt, k_t[0]).then_inc(kt_lo, 1)
                if exists(b):
                    scale_out(0, b)
                    dve.wait_ge(o_relu[0], b + 1)
                    nc.vector.tensor_tensor(x_now, x_now, o_buf[:, 0, :, :], ALU.add).then_inc(x1_done, 1)
                    dve.wait_ge(x1_done, b + 1)
                    norm_stats(1, b, x_now)
                if exists(b - 1):
                    dve.wait_ge(kp_done, b)
                    nc.vector.tensor_tensor(x_last, x_last, ps_b[:, :, :], ALU.add).then_inc(x2_done, 1)
                    dve.wait_ge(x2_done, b)
                    norm_stats(2, b - 1, x_last)
                if exists(b):
                    normalise(1, b, x_now)
                if exists(b - 1):
                    normalise(2, b - 1, x_last)
                if exists(b - 2):
                    scale_out(1, b - 2)
                if exists(b - 1):
                    h_low(2, b - 1)
                if exists(b):
                    dve.wait_ge(ht_hi, b + 1)
                    nc.vector.scalar_tensor_tensor(h_t[1][:, :, :].rearrange("p t c -> p (t c)"),
                                                   ps_c[:, :, :].rearrange("p q c -> p (q c)"), 0.0,
                                                   h_t[0][:, :, :].bitcast(F32).rearrange("p t c -> p (t c)"),
                                                   ALU.max, ALU.subtract).then_inc(ht_lo, 1)
                if exists(b - 1):
                    dve.wait_ge(l2_done, b)
                    dve.wait_ge(x_bias, b)
                    if later(b - 1):
                        dve.wait_ge(x4_done, b - 1)
                    nc.vector.tensor_tensor(x_b[:, :, :], x_last, ps_b[:, :, :], ALU.add).then_inc(x3_done, 1)
                    dve.wait_ge(x3_done, b)
                    norm_stats(3, b - 1, x_b)
                    normalise(3, b - 1, x_b)
                if exists(b + 1):
                    next_k, next_turn = (1, turn) if k == 0 else (0, turn + 1)
                    dve.wait_ge(loaded[next_k], 16 * next_turn + 16)
                    norm_stats(0, b + 1, x_next)
                if exists(b):
                    dve.wait_ge(zl_hi, b + 1)
                    low(z_l[1][:, :, :], ps_zl, z_l[0][:, :, :]).then_inc(zl_lo, 1)
                if exists(b - 1):
                    h_low(3, b - 1)
                if exists(b + 1):
                    normalise(0, b + 1, x_next)
                if exists(b):
                    dve.wait_ge(zg_hi, b + 1)
                    low(z_g[1][:, :, :], ps_zg, z_g[0][:, :, :]).then_inc(zg_lo, 1)
                if exists(b + 1):
                    h_low(0, b + 1)

            setup()
            steps(dve, body)

        @block.gpsimd
        def _(pool):
            def setup():
                nc.gpsimd.memset(ident[:, :], 0.0).then_inc(setup_ident, 1)
                pool.wait_ge(setup_ident, 1)
                nc.gpsimd.affine_select(out=ident[:, :], in_=ident[:, :], compare_op=ALU.not_equal, fill=1.0,
                                        base=0, pattern=[[-1, P]], channel_multiplier=1).then_inc(setup_ident, 1)
                pool.wait_ge(setup_const, 1)
                pool.wait_ge(setup_load[0], SMALL_LOADS * 16)

            def largest_query(a, e):
                pool.wait_ge(q_maxed[a], e + 1)
                if later(e):
                    pool.wait_ge(row_clamped[a], e)
                pool.sem_inc(pool_go, 1)
                nc.gpsimd.partition_all_reduce(q_max[:, a:a + 1], q_max1[:, a:a + 1], P, bass.bass_isa.ReduceOp.max).then_inc(q_all[a], 1)

            def e_low(a, e):
                pool.wait_ge(e_hi_23[a], e + 1)
                nc.gpsimd.tensor_tensor(e_hl[a][1][:, 2:4, :], e_full[:, 2:4, :], e_hl[a][0][:, 2:4, :].bitcast(F32),
                                        ALU.subtract).then_inc(e_lo_23[a], 1)

            def deviation(layer, e):
                pool.wait_ge(mean_var_done[layer], e + 1)
                if later(e):
                    pool.wait_ge(rstd_done[layer], e)
                nc.gpsimd.tensor_tensor(var_eps[:, layer, :], mean_var[:, layer, :, 1], eps_col[:, :],
                                        ALU.add).then_inc(var_eps_done[layer], 1)
                pool.wait_ge(var_eps_done[layer], e + 1)
                if later(e):
                    pool.wait_ge(norm_done[layer], e)
                nc.gpsimd.tensor_tensor(rstd[:, layer, :], var_eps[:, layer, :], mhalf_col[:, :],
                                        ALU.pow).then_inc(rstd_done[layer], 1)

            def body(b, k, turn):
                x_last = x_a[:, 1 - k, :, :]
                if exists(b - 2):
                    largest_query(1, b - 2)
                    e_low(1, b - 2)
                if exists(b):
                    largest_query(0, b)
                    e_low(0, b)
                if exists(b - 1):
                    pool.wait_ge(norm_clamped, b)
                    if later(b - 1):
                        pool.wait_ge(degrees, b - 1)
                    nc.gpsimd.tensor_tensor(inv_norm[:, :], norm2[:, :], mhalf_col[:, :], ALU.pow).then_inc(norm_inv, 1)
                if exists(b):
                    deviation(1, b)
                if exists(b - 1):
                    deviation(2, b - 1)
                    pool.wait_ge(norm_done[2], b)
                    for t in range(CT):
                        last = nc.gpsimd.tensor_tensor(x_last[:, t, :], x_last[:, t, :], bias_row[:, :], ALU.add)
                    last.then_inc(x_bias, 1)
                if exists(b - 2):
                    pool.wait_ge(o_relu[1], b - 1)
                    nc.gpsimd.tensor_tensor(o_buf[:, 1, :, :], o_buf[:, 1, :, :], x_b[:, :, :], ALU.add).then_inc(x4_done, 1)
                if exists(b - 1):
                    deviation(3, b - 1)
                if exists(b + 1):
                    deviation(0, b + 1)

            setup()
            steps(pool, body)


_INPUTS = ["x", "adj", "L0_gnn_wq", "L0_gnn_wk", "L0_gnn_bm", "L1_gnn_W_lang", "L1_gnn_W_grav", "L1_gnn_W_V",
           "L1_gnn_W_O", "L1_gnn_gate_logit", "L1_gnn_log_sigma", "L2_gnn_bias", "L3_gnn_wq", "L3_gnn_wk", "L3_gnn_bm"]


def kernel(**inputs):
    import numpy as np
    import concourse.bacc as bacc
    from concourse.bass_utils import run_bass_kernel_spmd

    nc = bacc.Bacc("TRN2", target_bir_lowering=False, num_devices=1)
    arrays, args = {}, []
    for name in _INPUTS:
        a = np.ascontiguousarray(inputs[name])
        if a.ndim == 0:
            a = a.reshape(1)
        arrays[f"in_{name}"] = a
        args.append(nc.dram_tensor(f"in_{name}", a.shape, mybir.dt.from_np(a.dtype), kind="ExternalInput").ap())
    out = nc.dram_tensor("out", arrays["in_x"].shape, F32, kind="ExternalOutput").ap()
    emit(nc, *args, out)
    r = run_bass_kernel_spmd(nc, [arrays], core_ids=[0])
    return r.results[0]["out"]
```

```python
from contextlib import ExitStack

import concourse.bass as bass
from concourse import mybir

F32 = mybir.dt.float32
F32R = mybir.dt.float32r
ALU = mybir.AluOpType
ACT = mybir.ActivationFunctionType
AX = mybir.AxisListType

P = 128
LN_EPS = 1e-5
NORM_EPS = 1e-8
SLOPE = 0.01
FIRST_LOOPED = 4
SMALL_LOADS = 10


def emit(nc, x, adj, wq0, wk0, bm0, w_lang, w_grav, w_v, w_o, gate, log_sigma, bias2, wq3, wk3, bm3, out):
    B, C, N = x.shape
    CT = C // P
    NT = N // P
    D = N
    DT = D // P
    YC = C + 2
    assert B % 2 == 0 and B > FIRST_LOOPED and NT == 4 and CT == 2

    x_view = x.rearrange("b (t p) n -> b p t n", p=P)
    out_view = out.rearrange("b (t p) n -> b p t n", p=P)

    ctx = ExitStack()
    with ctx:
        def sb(name, shape, dt=F32):
            return ctx.enter_context(nc.sbuf_tensor(name, shape, dt))

        def ps(name, shape):
            return ctx.enter_context(nc.psum_tensor(name, shape, F32))

        def split(name, shape):
            return sb(name + "_hi", shape, F32R), sb(name + "_lo", shape, F32R)

        ident = sb("ident", [P, P])
        off_diag = sb("off_diag", [P, P])
        ones = sb("ones", [P, P])
        wy = split("wy", [P, CT, YC])
        wk_rep = [split(f"wk_rep{a}", [P, CT, P]) for a in range(2)]
        wqk_col = sb("wqk_col", [P, 2, 2, CT])
        wqk = split("wqk", [P, 2, 2, CT])
        bm_col = sb("bm_col", [P, 2, CT])
        adj_off = sb("adj_off", [P, CT, C])
        w2 = split("w2", [P, CT, C])
        bias_row = sb("bias_row", [P, N])
        lang_t = split("lang_t", [P, DT, D])
        grav_t = split("grav_t", [P, DT, D])
        vo_t = split("vo_t", [P, DT, D])
        scal = sb("scal", [P, 6])
        eps_col = sb("eps_col", [P, CT])
        mhalf_col = sb("mhalf_col", [P, CT])
        inv_var = scal[:, 2:3]
        w_l = scal[:, 5:6]

        x_a = sb("x_a", [P, 2, CT, N])
        x_b = sb("x_b", [P, 2, CT, N])
        norm = sb("norm", [P, CT, N])
        h_a = split("h_a", [P, CT, N])
        h_b = split("h_b", [P, CT, N])
        stats = sb("stats", [P, 4, CT, 6])
        mean_var = sb("mean_var", [P, 4, CT, 2])
        var_eps = sb("var_eps", [P, 4, CT])
        rstd = sb("rstd", [P, 4, CT])
        y = [split(f"y{a}", [P, NT, C]) for a in range(2)]
        q_col = sb("q_col", [P, 2, NT])
        q_max1 = sb("q_max1", [P, 2])
        q_max = sb("q_max", [P, 2])
        q_min = sb("q_min", [P, 2])
        q_sub = sb("q_sub", [P, 2, NT])
        exp_q = sb("exp_q", [P, 2, NT])
        q_slope = sb("q_slope", [P, 2, NT])
        u_row = sb("u_row", [P, N])
        v_row = sb("v_row", [P, N])
        e_full = sb("e_full", [P, NT, N])
        e_sum = sb("e_sum", [P, 2, N])
        e_hl = [split(f"e{a}", [P, NT, N]) for a in range(2)]
        rec = sb("rec", [P, N])
        o_buf = sb("o_buf", [P, 2, CT, N])
        h_t = split("h_t", [P, DT, C])
        z_l = split("z_l", [P, DT, C])
        z_g = split("z_g", [P, DT, C])
        pv = [t[:, :, :].rearrange("p (n q) c -> p n (q c)", n=CT) for t in z_l]
        k_t = [t[:, 0:CT, :] for t in z_g]
        diag_l = sb("diag_l", [P, CT, P])
        diag_g = sb("diag_g", [P, CT, P])
        diag_n = sb("diag_n", [P, CT, P])
        norm2 = sb("norm2", [P, CT])
        inv_norm = sb("inv_norm", [P, CT])
        half_sq = sb("half_sq", [P, CT])
        mix_l = sb("mix_l", [P, CT, C])
        mix_g = sb("mix_g", [P, CT, C])
        degree = sb("degree", [P, 2 * CT])
        degree_inv = sb("degree_inv", [P, 2 * CT])
        coef = sb("coef", [P, 2 * CT])
        weight = sb("weight", [P, 2 * CT])
        room = [x_a[:, :, :, :].rearrange("p a t n -> p (a t) n"), o_buf[:, :, :, :].rearrange("p a t n -> p (a t) n")]
        adj_in = norm[:, 0, :].rearrange("p (t c) -> p t c", t=CT)
        w_o_t = e_full
        w2_full = mix_l

        ps_a = ps("ps_a", [P, 2, 512])
        ps_b = ps("ps_b", [P, 2, 512])
        ps_c = ps("ps_c", [P, 2, 512])
        ps_6 = ps("ps_6", [P, 512])
        ps_7 = ps("ps_7", [P, 512])
        ps_y = [ps_a, ps_c]
        ps_keys = [ps_7, ps_6]
        ps_sums = ps_6
        ps_o = [ps_c, ps_a]
        ps_zl = ps_a[:, :, :].rearrange("p q (t c) -> p (q t) c", t=2)
        ps_zg = ps_c[:, :, :].rearrange("p q (t c) -> p (q t) c", t=2)
        ps_ht = ps_zg
        gram_l = ps_b[:, 0, :].rearrange("p (t c) -> p t c", t=CT)
        gram_g = ps_b[:, 1, :].rearrange("p (t c) -> p t c", t=CT)
        ps_kt = ps_7[:, :].rearrange("p (t c) -> p t c", t=CT)
        ps_setup = [ps_a, ps_b, ps_c]

        def diagonal_blocks(bank):
            return bank.rearrange("p (u w) -> p u w", w=P)[:, 0:4:3, :]

        def one(name):
            return ctx.enter_context(nc.semaphore(name))

        def by_attention(name):
            return [one(f"{name}_{a}") for a in range(2)]

        def by_half(name):
            return [one(f"{name}_{n}") for n in range(2)]

        def by_layer(name):
            return [one(f"{name}_{layer}") for layer in range(4)]

        setup_const = one("setup_const")
        setup_ident = one("setup_ident")
        setup_pe = one("setup_pe")
        setup_hi = one("setup_hi")
        setup_lo = one("setup_lo")
        setup_dve = one("setup_dve")
        setup_scal = one("setup_scal")
        stored = one("stored")
        pv_done = by_half("pv_done")
        gram_done = one("gram_done")
        sq_added = one("sq_added")
        norms_spread = one("norms_spread")
        kt_done = one("kt_done")
        kp_done = one("kp_done")
        ht_done = one("ht_done")
        zl_done = one("zl_done")
        zg_done = one("zg_done")
        l2_done = one("l2_done")
        diags = one("diags")
        norms2 = one("norms2")
        norm_clamped = one("norm_clamped")
        norm_inv = one("norm_inv")
        norm_diag = one("norm_diag")
        grav_arg = one("grav_arg")
        grav_exp = one("grav_exp")
        adj_scale = one("adj_scale")
        mixed_l = one("mixed_l")
        mixed_g = one("mixed_g")
        degrees = one("degrees")
        deg_max = one("deg_max")
        deg_inv = one("deg_inv")
        weighted = one("weighted")
        coefs = one("coefs")
        grav_part = one("grav_part")
        k_done = one("k_done")
        kt_hi = one("kt_hi")
        kt_lo = one("kt_lo")
        pv_hi = by_half("pv_hi")
        pv_lo = by_half("pv_lo")
        ht_hi = by_half("ht_hi")
        ht_lo = by_half("ht_lo")
        zl_hi = one("zl_hi")
        zl_lo = one("zl_lo")
        zg_hi = one("zg_hi")
        zg_lo = one("zg_lo")
        x1_done = one("x1_done")
        x2_done = one("x2_done")
        x_bias = one("x_bias")
        x3_done = one("x3_done")
        x4_done = one("x4_done")
        dve_go = one("dve_go")
        pool_go = one("pool_go")
        y_done = by_attention("y_done")
        keys_done = by_attention("keys_done")
        sums_done = by_attention("sums_done")
        o_done = by_attention("o_done")
        q_read = by_attention("q_read")
        q_maxed = by_attention("q_maxed")
        q_all = by_attention("q_all")
        q_subbed = by_attention("q_subbed")
        exp_q_done = by_attention("exp_q_done")
        y_hi_01 = by_attention("y_hi_01")
        y_hi_23 = by_attention("y_hi_23")
        y_lo_01 = by_attention("y_lo_01")
        y_lo = by_attention("y_lo")
        row_clamped = by_attention("row_clamped")
        row_exped = by_attention("row_exped")
        e_v = by_attention("e_v")
        e_01 = by_attention("e_01")
        e_23 = by_attention("e_23")
        e_hi_01 = by_attention("e_hi_01")
        e_hi_23 = by_attention("e_hi_23")
        e_lo_01 = by_attention("e_lo_01")
        e_lo_23 = by_attention("e_lo_23")
        e_part_sum = by_attention("e_part_sum")
        e_summed = by_attention("e_summed")
        log_sum = by_attention("log_sum")
        rec_done = by_attention("rec_done")
        o_scaled = by_attention("o_scaled")
        o_relu = by_attention("o_relu")
        stats_done = by_layer("stats_done")
        mean_var_done = by_layer("mean_var_done")
        var_eps_done = by_layer("var_eps_done")
        rstd_done = by_layer("rstd_done")
        norm_done = by_layer("norm_done")
        h_hi = by_layer("h_hi")
        h_lo = by_layer("h_lo")
        loaded = [one(f"loaded_{k}") for k in range(2)]
        setup_load = [one(f"setup_load_{k}") for k in range(3)]

        def steps(eng, body):
            for b in range(-1, FIRST_LOOPED):
                body(b, b % 2, b // 2)
            with eng.Fori(FIRST_LOOPED // 2, B // 2 - 1) as turn:
                body(2 * turn, 0, turn)
                body(2 * turn + 1, 1, turn)
            for b in range(B - 2, B + 2):
                body(b, b % 2, b // 2)

        def exists(e):
            return not isinstance(e, int) or 0 <= e < B

        def later(e):
            return not isinstance(e, int) or e > 0

        def other_e_used(eng, a, e, step):
            if a == 1 and exists(e + 2):
                eng.wait_ge(step[0], e + 3)
            elif a == 1 and later(e):
                eng.wait_ge(step[1], e)
            if a == 0 and later(e - 2):
                eng.wait_ge(step[1], e - 2)
            elif a == 0 and later(e):
                eng.wait_ge(step[0], e)

        block = ctx.enter_context(nc.Block())

        @block.sync
        def _(sp):
            sp.dma_start(adj_in, adj.rearrange("(t p) c -> p t c", p=P)).then_inc(setup_load[0], 16)
            for a, (wq, wk, bm) in enumerate(((wq0, wk0, bm0), (wq3, wk3, bm3))):
                sp.dma_start(wqk_col[:, a, 0, :], wq.rearrange("(t p) -> p t", p=P), allow_slow_non_contiguous=True).then_inc(setup_load[0], 16)
                sp.dma_start(wqk_col[:, a, 1, :], wk.rearrange("(t p) -> p t", p=P), allow_slow_non_contiguous=True).then_inc(setup_load[0], 16)
                sp.dma_start(bm_col[:, a, :], bm.rearrange("(t p) -> p t", p=P), allow_slow_non_contiguous=True).then_inc(setup_load[0], 16)
            sp.dma_start(scal[:, 0:1], gate.partition_broadcast(P)).then_inc(setup_load[0], 16)
            sp.dma_start(scal[:, 1:2], log_sigma.partition_broadcast(P)).then_inc(setup_load[0], 16)
            sp.dma_start(bias_row[:, :], bias2.partition_broadcast(P)).then_inc(setup_load[0], 16)
            for n, w in enumerate((w_lang, w_grav, w_o, w_v)):
                if n >= 2:
                    sp.wait_ge(setup_pe, 1 + 2 * (n - 1))
                sp.dma_start(room[n % 2], w.rearrange("(t p) d -> p t d", p=P)).then_inc(setup_load[1 + n % 2], 16)

            def body(b, k, turn):
                next_k, next_turn = (1, turn) if k == 0 else (0, turn + 1)
                if exists(b + 1):
                    if later(b):
                        sp.wait_ge(x2_done, b)
                    else:
                        sp.wait_ge(setup_pe, 7)
                    sp.dma_start(x_a[:, next_k, :, :], x_view[b + 1]).then_inc(loaded[next_k], 16)
                if exists(b - 2):
                    sp.wait_ge(x4_done, b - 1)
                    sp.dma_start(out_view[b - 2], o_buf[:, 1, :, :]).then_inc(stored, 16)

            steps(sp, body)
            sp.wait_ge(stored, 16 * B)

        @block.tensor
        def _(pe):
            def passes(out, left, right, start, stop):
                nc.tensor.matmul(out, left[0], right[0], start=start, stop=False, skip_group_check=True)
                nc.tensor.matmul(out, left[0], right[1], start=False, stop=False, skip_group_check=True)
                return nc.tensor.matmul(out, left[1], right[0], start=False, stop=stop, skip_group_check=True)

            def transposed(bank_pair, w, half):
                for q in range(2):
                    for t in range(DT):
                        c = (2 * half + q) * P
                        last = nc.tensor.transpose(bank_pair[:, q, t * P:(t + 1) * P], w[:, t, c:c + P], ident[:, :])
                return last

            def setup():
                pe.wait_ge(setup_load[0], SMALL_LOADS * 16)
                pe.wait_ge(setup_ident, 2)
                for t in range(CT):
                    for o in range(CT):
                        last = nc.tensor.transpose(ps_6[:, t * C + o * P:t * C + (o + 1) * P],
                                                   adj_in[:, o, t * P:(t + 1) * P], ident[:, :])
                last.then_inc(setup_pe, 1)
                pe.wait_ge(setup_load[1], 16)
                transposed(ps_a, room[0], 0).then_inc(setup_pe, 1)
                transposed(ps_b, room[0], 1).then_inc(setup_pe, 1)
                pe.wait_ge(setup_load[2], 16)
                transposed(ps_c, room[1], 0).then_inc(setup_pe, 1)
                pe.wait_ge(setup_lo, 2)
                transposed(ps_a, room[1], 1).then_inc(setup_pe, 1)
                pe.wait_ge(setup_load[1], 32)
                pe.wait_ge(setup_lo, 3)
                transposed(ps_b, room[0], 0).then_inc(setup_pe, 1)
                pe.wait_ge(setup_lo, 4)
                transposed(ps_c, room[0], 1).then_inc(setup_pe, 1)
                pe.wait_ge(setup_load[2], 32)
                pe.wait_ge(setup_hi, 7)
                pe.wait_ge(setup_lo, 5)
                for half, pair in ((0, ps_a), (1, ps_b)):
                    for q in range(2):
                        c = (2 * half + q) * P
                        for t in range(DT):
                            last = nc.tensor.matmul(pair[:, q, :], room[1][:, t, c:c + P], w_o_t[:, t, :],
                                                    start=(t == 0), stop=(t == DT - 1))
                    last.then_inc(setup_pe, 1)

            def project(a, e):
                h = (h_a, h_b)[a]
                pe.wait_ge(h_lo[(0, 3)[a]], e + 1)
                if a == 0 and later(e):
                    pe.wait_ge(zl_lo, e)
                if a == 1 and exists(e + 2):
                    pe.wait_ge(y_lo[0], e + 3)
                elif a == 1 and exists(e + 1):
                    pe.wait_ge(zg_lo, e + 2)
                elif a == 1:
                    pe.wait_ge(o_scaled[1], e)
                for n in range(NT):
                    if a == 0 and n == 2 and later(e):
                        pe.wait_ge(zg_lo, e)
                    for t in range(CT):
                        last = passes(ps_y[n // 2][:, n % 2, 0:YC],
                                      [x[:, t, n * P:(n + 1) * P] for x in h], [w[:, t, :] for w in wy],
                                      t == 0, t == CT - 1)
                last.then_inc(y_done[a], 1)
                if a == 0 and later(e - 1):
                    pe.wait_ge(kt_lo, e - 1)
                if a == 1 and later(e):
                    pe.wait_ge(log_sum[1], e)
                for t in range(CT):
                    last = passes(ps_keys[a][:, :], [w[:, t, :] for w in wk_rep[a]], [x[:, t, :] for x in h],
                                  t == 0, t == CT - 1)
                last.then_inc(keys_done[a], 1)

            def attend(a, e):
                pe.wait_ge(y_lo[a], e + 1)
                if a == 0 and later(e - 1):
                    pe.wait_ge(y_lo[1], e - 1)
                for o, half in ((0, 0), (1, 0), (0, 1), (1, 1)):
                    pe.wait_ge((e_lo_01, e_lo_23)[half][a], e + 1)
                    if a == 1 and half == 0 and exists(e + 1):
                        pe.wait_ge(pv_lo[o], e + 2)
                    for n in (2 * half, 2 * half + 1):
                        last = passes(ps_o[a][:, o, :], [v[:, n, o * P:(o + 1) * P] for v in y[a]],
                                      [v[:, n, :] for v in e_hl[a]], n == 0, n == NT - 1)
                    if o == 0 and half == 1:
                        pe.wait_ge(e_summed[a], e + 1)
                        if a == 0 and later(e - 1):
                            pe.wait_ge(row_clamped[1], e - 1)
                        elif a == 0 and later(e):
                            pe.wait_ge(log_sum[0], e)
                        if a == 1 and exists(e + 2):
                            pe.wait_ge(log_sum[0], e + 3)
                        nc.tensor.matmul(ps_sums[:, :], ones[:, :], e_sum[:, a, :], start=True,
                                         stop=True).then_inc(sums_done[a], 1)
                last.then_inc(o_done[a], 1)

            def grams(e):
                pe.wait_ge(zg_lo, e + 1)
                if later(e):
                    pe.wait_ge(x3_done, e)
                for gram, z in ((gram_l, z_l), (gram_g, z_g)):
                    for n in range(CT):
                        for t in range(DT):
                            last = passes(gram[:, n, :], [v[:, t, n * P:(n + 1) * P] for v in z],
                                          [v[:, t, :] for v in z], n == 0 and t == 0, t == DT - 1)
                last.then_inc(gram_done, 1)

            def add_lengths(e):
                pe.wait_ge(diags, e + 1)
                for n in range(CT):
                    last = nc.tensor.matmul(gram_g[:, n, :], ones[:, :], diag_g[:, :, :].rearrange("p t c -> p (t c)"),
                                            start=False, stop=True, skip_group_check=True)
                last.then_inc(sq_added, 1)

            def spread_norms(e):
                pe.wait_ge(norm_diag, e + 1)
                if exists(e + 1):
                    pe.wait_ge(row_clamped[0], e + 2)
                elif later(e):
                    pe.wait_ge(kt_lo, e)
                nc.tensor.matmul(ps_7[:, 0:C], ones[:, :], diag_n[:, :, :].rearrange("p t c -> p (t c)"),
                                 start=True, stop=True).then_inc(norms_spread, 1)

            def values(n, e):
                if n == 0 and later(e):
                    pe.wait_ge(y_lo_01[1], e)
                elif n == 0 and exists(e + 1):
                    pe.wait_ge(y_lo[0], e + 2)
                for t in range(DT):
                    last = passes(ps_a[:, n, :], [v[:, t, n * P:(n + 1) * P] for v in h_t],
                                  [w[:, t, :] for w in vo_t], t == 0, t == DT - 1)
                last.then_inc(pv_done[n], 1)

            def turn_mixing(e):
                pe.wait_ge(k_done, e + 1)
                for t in range(CT):
                    for n in range(CT):
                        last = nc.tensor.transpose(ps_kt[:, t, n * P:(n + 1) * P], mix_l[:, n, t * P:(t + 1) * P],
                                                   ident[:, :])
                last.then_inc(kt_done, 1)

            def mix(n, e):
                pe.wait_ge(kt_lo, e + 1)
                pe.wait_ge(pv_lo[1], e + 1)
                for t in range(CT):
                    last = passes(ps_b[:, n, :], [v[:, t, n * P:(n + 1) * P] for v in k_t],
                                  [v[:, t, :] for v in pv], t == 0, t == CT - 1)
                if n == CT - 1:
                    last.then_inc(kp_done, 1)

            def turn_h(e):
                pe.wait_ge(norm_done[1], e + 1)
                for t in range(DT):
                    for n in range(CT):
                        last = nc.tensor.transpose(ps_ht[:, t, n * P:(n + 1) * P], norm[:, n, t * P:(t + 1) * P],
                                                   ident[:, :])
                last.then_inc(ht_done, 1)

            def fixed(e):
                pe.wait_ge(h_lo[2], e + 1)
                for m in range(CT):
                    for n in range(CT):
                        last = passes(ps_b[:, m, :], [w[:, n, m * P:(m + 1) * P] for w in w2],
                                      [v[:, n, :] for v in h_b], n == 0, n == CT - 1)
                last.then_inc(l2_done, 1)

            def z_of(target, weight_t, e, done):
                for o in range(DT):
                    for t in range(DT):
                        if o == 0 and t % 2 == 0:
                            pe.wait_ge(ht_lo[t // 2], e + 1)
                        last = passes(target[:, o, :], [w[:, t, o * P:(o + 1) * P] for w in weight_t],
                                      [v[:, t, :] for v in h_t], o % 2 == 0 and t == 0, t == DT - 1)
                last.then_inc(done, 1)

            def body(b, k, turn):
                if exists(b):
                    project(0, b)
                if exists(b - 1):
                    grams(b - 1)
                if exists(b - 2):
                    project(1, b - 2)
                if exists(b - 1):
                    add_lengths(b - 1)
                    spread_norms(b - 1)
                    values(0, b - 1)
                if exists(b):
                    attend(0, b)
                if exists(b - 1):
                    values(1, b - 1)
                    turn_mixing(b - 1)
                if exists(b - 2):
                    attend(1, b - 2)
                if exists(b - 1):
                    mix(0, b - 1)
                if exists(b):
                    turn_h(b)
                if exists(b - 1):
                    mix(1, b - 1)
                if exists(b):
                    if later(b - 1):
                        pe.wait_ge(o_scaled[1], b - 1)
                    elif later(b):
                        pe.wait_ge(pv_lo[1], b)
                    z_of(ps_zl, lang_t, b, zl_done)
                    z_of(ps_zg, grav_t, b, zg_done)
                if exists(b - 1):
                    fixed(b - 1)

            setup()
            steps(pe, body)

        @block.scalar
        def _(act):
            def setup():
                nc.scalar.preload_act_table_set("natural_log_exp_and_others")
                act.wait_ge(setup_load[0], SMALL_LOADS * 16)
                nc.scalar.activation(scal[:, 2:3], scal[:, 1:2], ACT.Exp, scale=-2.0)
                nc.scalar.activation(scal[:, 3:4], scal[:, 0:1], ACT.Exp, scale=-1.0)
                nc.scalar.copy(wqk[0][:, :, :, :], wqk_col[:, :, :, :]).then_inc(setup_scal, 1)
                act.wait_ge(setup_pe, 1)
                nc.scalar.copy(wy[0][:, :, 0:C], ps_6[:, :].rearrange("p (t c) -> p t c", t=CT)).then_inc(setup_hi, 1)
                for n in range(8):
                    act.wait_ge(setup_pe, n + 2)
                    rows = slice(2 * (n % 2), 2 * (n % 2) + 2)
                    target = (lang_t[0], grav_t[0], w_o_t, vo_t[0])[n // 2]
                    source = (ps_a, ps_b, ps_c, ps_a, ps_b, ps_c, ps_a, ps_b)[n]
                    nc.scalar.copy(target[:, rows, :], source[:, :, :]).then_inc(setup_hi, 1)

            def y_high(a, e):
                act.wait_ge(y_done[a], e + 1)
                if later(e):
                    act.wait_ge(q_subbed[a], e)
                    act.wait_ge(o_done[a], e)
                for g in range(2):
                    last = nc.scalar.copy(q_col[:, a, 2 * g:2 * g + 2], ps_y[g][:, :, C + a])
                last.then_inc(q_read[a], 1)
                nc.scalar.copy(y[a][0][:, 0:2, :], ps_y[0][:, :, 0:C]).then_inc(y_hi_01[a], 1)
                nc.scalar.copy(y[a][0][:, 2:4, :], ps_y[1][:, :, 0:C]).then_inc(y_hi_23[a], 1)

            def exponentials(a, e):
                act.wait_ge(q_subbed[a], e + 1)
                if later(e):
                    act.wait_ge(e_23[a], e)
                nc.scalar.activation(exp_q[:, a, :], q_sub[:, a, :], ACT.Exp).then_inc(exp_q_done[a], 1)
                act.wait_ge(keys_done[a], e + 1)
                other_e_used(act, a, e, e_23)
                nc.scalar.activation(u_row[:, :], ps_keys[a][:, :], ACT.Relu, bias=q_min[:, a:a + 1], scale=-1.0)
                nc.scalar.activation(v_row[:, :], ps_keys[a][:, :], ACT.Relu,
                                     bias=q_max[:, a:a + 1]).then_inc(row_clamped[a], 1)
                act.wait_ge(row_clamped[a], e + 1)
                nc.scalar.activation(u_row[:, :], u_row[:, :], ACT.Exp, scale=SLOPE - 1.0).then_inc(row_exped[a], 1)

            def slope_exponentials(a, e):
                other_e_used(act, a, e, e_summed)
                other_e_used(act, a, e, e_lo_01)
                other_e_used(act, a, e, e_lo_23)
                for n in range(NT):
                    nc.scalar.activation(e_full[:, n, :], v_row[:, :], ACT.Exp, bias=q_slope[:, a, n:n + 1],
                                         scale=SLOPE - 1.0).then_inc(e_v[a], 1)

            def value_high(n, e):
                act.wait_ge(pv_done[n], e + 1)
                nc.scalar.copy(pv[0][:, n, :], ps_a[:, n, :]).then_inc(pv_hi[n], 1)

            def e_high_01(a, e):
                act.wait_ge(e_01[a], e + 1)
                nc.scalar.copy(e_hl[a][0][:, 0:2, :], e_full[:, 0:2, :]).then_inc(e_hi_01[a], 1)

            def e_high_23(a, e):
                act.wait_ge(e_23[a], e + 1)
                nc.scalar.copy(e_hl[a][0][:, 2:4, :], e_full[:, 2:4, :]).then_inc(e_hi_23[a], 1)

            def inverse_sums(a, e):
                act.wait_ge(sums_done[a], e + 1)
                if a == 0 and later(e - 2):
                    act.wait_ge(o_scaled[1], e - 2)
                elif a == 0 and later(e):
                    act.wait_ge(o_scaled[0], e)
                if a == 1 and exists(e + 2):
                    act.wait_ge(o_scaled[0], e + 3)
                elif a == 1 and later(e):
                    act.wait_ge(o_scaled[1], e)
                nc.scalar.activation(rec[:, :], ps_sums[:, :], ACT.Ln).then_inc(log_sum[a], 1)
                act.wait_ge(log_sum[a], e + 1)
                nc.scalar.activation(rec[:, :], rec[:, :], ACT.Exp, scale=-1.0).then_inc(rec_done[a], 1)

            def biased_relu(a, e):
                act.wait_ge(o_scaled[a], e + 1)
                for o in range(CT):
                    last = nc.scalar.activation(o_buf[:, a, o, :], o_buf[:, a, o, :], ACT.Relu,
                                                bias=bm_col[:, a, o:o + 1])
                last.then_inc(o_relu[a], 1)

            def h_high(layer, e):
                act.wait_ge(norm_done[layer], e + 1)
                if layer == 0 and later(e):
                    act.wait_ge(keys_done[0], e)
                if layer == 2 and later(e):
                    act.wait_ge(keys_done[1], e)
                if layer == 3:
                    act.wait_ge(l2_done, e + 1)
                h = h_a if layer == 0 else h_b
                nc.scalar.activation(h[0][:, :, :], norm[:, :, :], ACT.Relu).then_inc(h_hi[layer], 1)

            def body(b, k, turn):
                if exists(b):
                    y_high(0, b)
                if exists(b - 2):
                    h_high(3, b - 2)
                if exists(b):
                    exponentials(0, b)
                    slope_exponentials(0, b)
                if exists(b - 2):
                    y_high(1, b - 2)
                if exists(b):
                    e_high_01(0, b)
                    e_high_23(0, b)
                if exists(b - 2):
                    exponentials(1, b - 2)
                if exists(b - 1):
                    act.wait_ge(grav_arg, b)
                    nc.scalar.activation(mix_g[:, :, :], mix_g[:, :, :], ACT.Exp, scale=inv_var).then_inc(grav_exp, 1)
                if exists(b - 1):
                    value_high(0, b - 1)
                if exists(b - 2):
                    slope_exponentials(1, b - 2)
                    e_high_01(1, b - 2)
                if exists(b):
                    inverse_sums(0, b)
                if exists(b - 1):
                    value_high(1, b - 1)
                if exists(b - 2):
                    e_high_23(1, b - 2)
                if exists(b):
                    biased_relu(0, b)
                if exists(b - 1):
                    act.wait_ge(kt_done, b)
                    nc.scalar.copy(k_t[0], ps_kt).then_inc(kt_hi, 1)
                if exists(b - 2):
                    inverse_sums(1, b - 2)
                if exists(b):
                    act.wait_ge(ht_done, b + 1)
                    if later(b):
                        act.wait_ge(pv_done[1], b)
                    for half in range(2):
                        rows = slice(2 * half, 2 * half + 2)
                        nc.scalar.activation(h_t[0][:, rows, :], ps_ht[:, rows, :], ACT.Relu).then_inc(ht_hi[half], 1)
                if exists(b - 2):
                    biased_relu(1, b - 2)
                if exists(b - 1):
                    h_high(2, b - 1)
                if exists(b):
                    act.wait_ge(zl_done, b + 1)
                    if later(b):
                        act.wait_ge(kp_done, b)
                    nc.scalar.copy(z_l[0][:, :, :], ps_zl).then_inc(zl_hi, 1)
                if exists(b + 1):
                    h_high(0, b + 1)
                if exists(b):
                    act.wait_ge(zg_done, b + 1)
                    nc.scalar.copy(z_g[0][:, :, :], ps_zg).then_inc(zg_hi, 1)

            setup()
            steps(act, body)

        @block.vector
        def _(dve):
            def low(out_lo, full, hi):
                return nc.vector.tensor_tensor(out_lo, full, hi.bitcast(F32), ALU.subtract)

            def setup():
                nc.vector.memset(eps_col[:, :], LN_EPS)
                nc.vector.memset(mhalf_col[:, :], -0.5)
                nc.vector.memset(ones[:, :], 1.0).then_inc(setup_const, 1)
                dve.wait_ge(setup_ident, 2)
                nc.vector.tensor_scalar(off_diag[:, :], ident[:, :], -1.0, 1.0, ALU.mult, ALU.add)
                dve.wait_ge(setup_scal, 1)
                low(wqk[1][:, :, :, :], wqk_col[:, :, :, :], wqk[0][:, :, :, :])
                nc.vector.tensor_scalar_add(scal[:, 4:5], scal[:, 3:4], 1.0).then_inc(setup_dve, 1)
                dve.wait_ge(setup_dve, 1)
                nc.vector.reciprocal(scal[:, 5:6], scal[:, 4:5])
                for a in range(2):
                    for half in range(2):
                        part = wqk[half][:, a, :, :].bitcast(F32)
                        for t in range(CT):
                            nc.vector.tensor_copy(wk_rep[a][half][:, t, :], part[:, 1, t:t + 1].to_broadcast([P, P]))
                            nc.vector.tensor_copy(wy[half][:, t, C + a:C + a + 1], part[:, 0, t:t + 1])
                nc.vector.tensor_tensor(w2_full[:, :, :], adj_in, adj_in, ALU.mult)
                for t in range(CT):
                    for c in range(CT):
                        block_of = lambda m: m[:, t, c * P:(c + 1) * P]
                        if t == c:
                            last = nc.vector.tensor_tensor(block_of(adj_off), block_of(adj_in), off_diag[:, :], ALU.mult)
                        else:
                            last = nc.vector.tensor_copy(block_of(adj_off), block_of(adj_in))
                last.then_inc(setup_dve, 1)
                dve.wait_ge(setup_dve, 2)
                nc.vector.tensor_scalar(weight[:, CT:2 * CT], w_l.to_broadcast([P, CT]), -1.0, 1.0, ALU.mult, ALU.add)
                nc.vector.tensor_copy(w2[0][:, :, :], w2_full[:, :, :]).then_inc(setup_dve, 1)
                dve.wait_ge(setup_dve, 3)
                low(w2[1][:, :, :], w2_full[:, :, :], w2[0][:, :, :])
                dve.wait_ge(setup_hi, 1)
                low(wy[1][:, :, 0:C], ps_6[:, :].rearrange("p (t c) -> p t c", t=CT), wy[0][:, :, 0:C]).then_inc(setup_lo, 1)
                for n in (0, 1, 2, 3, 6, 7):
                    dve.wait_ge(setup_hi, n + 2)
                    rows = slice(2 * (n % 2), 2 * (n % 2) + 2)
                    target = (lang_t, grav_t, None, vo_t)[n // 2]
                    source = (ps_a, ps_b, ps_c, ps_a, ps_b, ps_c, ps_a, ps_b)[n]
                    low(target[1][:, rows, :], source[:, :, :], target[0][:, rows, :]).then_inc(setup_lo, 1)

            def norm_stats(layer, e, x_in):
                for t in range(CT):
                    last = nc.vector.bn_stats(stats[:, layer, t, :], x_in[:, t, :])
                last.then_inc(stats_done[layer], 1)
                dve.wait_ge(stats_done[layer], e + 1)
                if later(e):
                    dve.wait_ge(norm_done[layer], e)
                dve.sem_inc(dve_go, 1)
                for t in range(CT):
                    last = nc.vector.bn_aggr(mean_var[:, layer, t, :], stats[:, layer, t, :])
                last.then_inc(mean_var_done[layer], 1)

            def normalise(layer, e, x_in):
                dve.wait_ge(rstd_done[layer], e + 1)
                if layer == 3 and exists(e + 2):
                    dve.wait_ge(h_lo[0], e + 3)
                elif layer == 3:
                    dve.wait_ge(h_lo[2], e + 1)
                if layer == 1 and later(e - 1):
                    dve.wait_ge(h_lo[3], e - 1)
                elif layer == 1:
                    dve.wait_ge(h_lo[0], e + 1)
                if layer == 2 and exists(e + 1):
                    dve.wait_ge(ht_done, e + 2)
                elif layer == 2:
                    dve.wait_ge(h_lo[3], e)
                if layer == 0 and later(e - 1):
                    dve.wait_ge(h_lo[2], e - 1)
                elif layer == 0 and later(e):
                    dve.wait_ge(h_lo[0], e)
                for t in range(CT):
                    last = nc.vector.tensor_scalar(norm[:, t, :], x_in[:, t, :], mean_var[:, layer, t, 0:1],
                                                   rstd[:, layer, t:t + 1], ALU.subtract, ALU.mult)
                last.then_inc(norm_done[layer], 1)

            def h_low(layer, e):
                dve.wait_ge(h_hi[layer], e + 1)
                h = h_a if layer == 0 else h_b
                nc.vector.scalar_tensor_tensor(h[1][:, :, :].rearrange("p t n -> p (t n)"),
                                               norm[:, :, :].rearrange("p t n -> p (t n)"), 0.0,
                                               h[0][:, :, :].bitcast(F32).rearrange("p t n -> p (t n)"),
                                               ALU.max, ALU.subtract).then_inc(h_lo[layer], 1)

            def queries(a, e):
                dve.wait_ge(q_read[a], e + 1)
                if later(e):
                    dve.wait_ge(q_all[a], e)
                nc.vector.reduce_max(q_max1[:, a:a + 1], q_col[:, a, :], axis=AX.X).then_inc(q_maxed[a], 1)

            def y_low(a, e):
                dve.wait_ge(y_hi_01[a], e + 1)
                low(y[a][1][:, 0:2, :], ps_y[0][:, :, 0:C], y[a][0][:, 0:2, :]).then_inc(y_lo_01[a], 1)
                dve.wait_ge(y_hi_23[a], e + 1)
                low(y[a][1][:, 2:4, :], ps_y[1][:, :, 0:C], y[a][0][:, 2:4, :]).then_inc(y_lo[a], 1)

            def shift_queries(a, e):
                dve.wait_ge(q_all[a], e + 1)
                if later(e):
                    dve.wait_ge(exp_q_done[a], e)
                    dve.wait_ge(row_clamped[a], e)
                    dve.wait_ge(e_v[a], NT * e)
                nc.vector.tensor_scalar(q_min[:, a:a + 1], q_max[:, a:a + 1], -1.0, None, ALU.mult)
                nc.vector.tensor_scalar(q_sub[:, a, :], q_col[:, a, :], q_max[:, a:a + 1], None, ALU.subtract)
                nc.vector.tensor_scalar(q_slope[:, a, :], q_col[:, a, :], q_max[:, a:a + 1], SLOPE, ALU.subtract,
                                        ALU.mult).then_inc(q_subbed[a], 1)

            def numerators(half, a, e):
                dve.wait_ge(exp_q_done[a], e + 1)
                dve.wait_ge(row_exped[a], e + 1)
                for n in (2 * half, 2 * half + 1):
                    dve.wait_ge(e_v[a], NT * e + n + 1)
                    last = nc.vector.scalar_tensor_tensor(e_full[:, n, :], u_row[:, :], exp_q[:, a, n:n + 1],
                                                          e_full[:, n, :], ALU.mult, ALU.max)
                last.then_inc((e_01, e_23)[half][a], 1)

            def e_low(a, e):
                dve.wait_ge(e_hi_23[a], e + 1)
                low(e_hl[a][1][:, 2:4, :], e_full[:, 2:4, :], e_hl[a][0][:, 2:4, :]).then_inc(e_lo_23[a], 1)

            def value_low(n, e):
                dve.wait_ge(pv_hi[n], e + 1)
                low(pv[1][:, n, :], ps_a[:, n, :], pv[0][:, n, :]).then_inc(pv_lo[n], 1)

            def gram_diagonals(e):
                dve.wait_ge(gram_done, e + 1)
                if later(e):
                    dve.wait_ge(sq_added, e)
                    dve.wait_ge(norms2, e)
                eye = ident[:, :].unsqueeze(1).to_broadcast([P, CT, P])
                nc.vector.tensor_tensor(diag_l[:, :, :], diagonal_blocks(ps_b[:, 0, :]), eye, ALU.mult)
                nc.vector.scalar_tensor_tensor(diag_g[:, :, :], diagonal_blocks(ps_b[:, 1, :]), -0.5, eye,
                                               ALU.mult, ALU.mult).then_inc(diags, 1)
                dve.wait_ge(diags, e + 1)
                nc.vector.reduce_sum(norm2[:, :], diag_l[:, :, :], axis=AX.X)
                nc.vector.reduce_sum(half_sq[:, :], diag_g[:, :, :], axis=AX.X).then_inc(norms2, 1)
                dve.wait_ge(norms2, e + 1)
                nc.vector.tensor_scalar_max(norm2[:, :], norm2[:, :], NORM_EPS * NORM_EPS).then_inc(norm_clamped, 1)

            def inverse_norms(e):
                dve.wait_ge(norm_inv, e + 1)
                if later(e):
                    dve.wait_ge(norms_spread, e)
                for t in range(CT):
                    last = nc.vector.tensor_scalar(diag_n[:, t, :], ident[:, :], inv_norm[:, t:t + 1], None, ALU.mult)
                last.then_inc(norm_diag, 1)
                if later(e):
                    dve.wait_ge(coefs, e)
                nc.vector.tensor_scalar(weight[:, 0:CT], inv_norm[:, :], w_l, None, ALU.mult).then_inc(weighted, 1)

            def gravity(e):
                dve.wait_ge(sq_added, e + 1)
                if later(e):
                    dve.wait_ge(k_done, e)
                for n in range(CT):
                    last = nc.vector.tensor_scalar(mix_g[:, n, :], gram_g[:, n, :], half_sq[:, n:n + 1], 0.0,
                                                   ALU.add, ALU.min)
                last.then_inc(grav_arg, 1)

            def mixing_kernels(e):
                dve.wait_ge(norms_spread, e + 1)
                if later(e):
                    dve.wait_ge(kt_done, e)
                nc.vector.tensor_tensor(mix_l[:, :, :], adj_off[:, :, :],
                                        ps_7[:, 0:C].unsqueeze(1).to_broadcast([P, CT, C]), ALU.mult).then_inc(adj_scale, 1)
                dve.wait_ge(adj_scale, e + 1)
                if later(e):
                    dve.wait_ge(deg_inv, e)
                for n in range(CT):
                    last = nc.vector.scalar_tensor_tensor(mix_l[:, n, :], gram_l[:, n, :], 0.0, mix_l[:, n, :],
                                                          ALU.max, ALU.mult, accum_out=degree[:, n:n + 1])
                last.then_inc(mixed_l, 1)
                dve.wait_ge(grav_exp, e + 1)
                for n in range(CT):
                    last = nc.vector.scalar_tensor_tensor(mix_g[:, n, :], mix_g[:, n, :], 1.0, adj_off[:, n, :],
                                                          ALU.mult, ALU.mult, accum_out=degree[:, CT + n:CT + n + 1])
                last.then_inc(mixed_g, 1)

            def mixing_sum(e):
                dve.wait_ge(mixed_g, e + 1)
                nc.vector.tensor_tensor(degree[:, 0:CT], degree[:, 0:CT], inv_norm[:, :], ALU.mult).then_inc(degrees, 1)
                dve.wait_ge(degrees, e + 1)
                nc.vector.tensor_scalar_max(degree[:, :], degree[:, :], NORM_EPS).then_inc(deg_max, 1)
                dve.wait_ge(deg_max, e + 1)
                nc.vector.reciprocal(degree_inv[:, :], degree[:, :]).then_inc(deg_inv, 1)
                dve.wait_ge(deg_inv, e + 1)
                nc.vector.tensor_tensor(coef[:, :], degree_inv[:, :], weight[:, :], ALU.mult).then_inc(coefs, 1)
                dve.wait_ge(coefs, e + 1)
                for n in range(CT):
                    last = nc.vector.tensor_scalar(mix_g[:, n, :], mix_g[:, n, :], coef[:, CT + n:CT + n + 1], None, ALU.mult)
                last.then_inc(grav_part, 1)
                dve.wait_ge(grav_part, e + 1)
                for n in range(CT):
                    last = nc.vector.scalar_tensor_tensor(mix_l[:, n, :], mix_l[:, n, :], coef[:, n:n + 1],
                                                          mix_g[:, n, :], ALU.mult, ALU.add)
                last.then_inc(k_done, 1)

            def scale_out(a, e):
                dve.wait_ge(rec_done[a], e + 1)
                dve.wait_ge(o_done[a], e + 1)
                if a == 0 and later(e):
                    dve.wait_ge(x1_done, e)
                if a == 1 and later(e):
                    dve.wait_ge(stored, 16 * e)
                nc.vector.tensor_tensor(o_buf[:, a, :, :], ps_o[a][:, :, :],
                                        rec[:, :].unsqueeze(1).to_broadcast([P, CT, N]), ALU.mult).then_inc(o_scaled[a], 1)

            def body(b, k, turn):
                x_now, x_other = x_a[:, k, :, :], x_a[:, 1 - k, :, :]
                x_b_old, x_b_last = x_b[:, k, :, :], x_b[:, 1 - k, :, :]
                if exists(b - 2):
                    dve.wait_ge(l2_done, b - 1)
                    dve.wait_ge(x_bias, b - 1)
                    nc.vector.tensor_tensor(x_b_old, x_b_old, ps_b[:, :, :], ALU.add).then_inc(x3_done, 1)
                    dve.wait_ge(x3_done, b - 1)
                    norm_stats(3, b - 2, x_b_old)
                if exists(b):
                    queries(0, b)
                if exists(b - 2):
                    normalise(3, b - 2, x_b_old)
                if exists(b):
                    y_low(0, b)
                if exists(b - 2):
                    h_low(3, b - 2)
                if exists(b):
                    shift_queries(0, b)
                if exists(b - 1):
                    gram_diagonals(b - 1)
                if exists(b):
                    numerators(0, 0, b)
                if exists(b - 1):
                    inverse_norms(b - 1)
                if exists(b - 2):
                    queries(1, b - 2)
                    y_low(1, b - 2)
                if exists(b):
                    numerators(1, 0, b)
                if exists(b - 2):
                    shift_queries(1, b - 2)
                if exists(b):
                    e_low(0, b)
                if exists(b - 1):
                    gravity(b - 1)
                if exists(b - 1):
                    mixing_kernels(b - 1)
                    value_low(0, b - 1)
                if exists(b - 2):
                    numerators(0, 1, b - 2)
                if exists(b - 1):
                    mixing_sum(b - 1)
                if exists(b - 2):
                    numerators(1, 1, b - 2)
                if exists(b):
                    scale_out(0, b)
                if exists(b - 1):
                    value_low(1, b - 1)
                if exists(b - 2):
                    e_low(1, b - 2)
                if exists(b):
                    dve.wait_ge(o_relu[0], b + 1)
                    nc.vector.tensor_tensor(x_now, x_now, o_buf[:, 0, :, :], ALU.add).then_inc(x1_done, 1)
                if exists(b - 1):
                    dve.wait_ge(kt_hi, b)
                    low(k_t[1], ps_kt, k_t[0]).then_inc(kt_lo, 1)
                if exists(b):
                    dve.wait_ge(x1_done, b + 1)
                    norm_stats(1, b, x_now)
                    normalise(1, b, x_now)
                if exists(b - 2):
                    scale_out(1, b - 2)
                if exists(b):
                    for half in range(2):
                        rows = slice(2 * half, 2 * half + 2)
                        dve.wait_ge(ht_hi[half], b + 1)
                        nc.vector.scalar_tensor_tensor(h_t[1][:, rows, :].rearrange("p t c -> p (t c)"),
                                                       ps_c[:, half, :], 0.0,
                                                       h_t[0][:, rows, :].bitcast(F32).rearrange("p t c -> p (t c)"),
                                                       ALU.max, ALU.subtract).then_inc(ht_lo[half], 1)
                if exists(b - 1):
                    dve.wait_ge(kp_done, b)
                    if later(b - 2):
                        dve.wait_ge(x4_done, b - 2)
                    nc.vector.tensor_tensor(x_b_last, x_other, ps_b[:, :, :], ALU.add).then_inc(x2_done, 1)
                    dve.wait_ge(x2_done, b)
                    norm_stats(2, b - 1, x_b_last)
                    normalise(2, b - 1, x_b_last)
                if exists(b + 1):
                    next_k, next_turn = (1, turn) if k == 0 else (0, turn + 1)
                    dve.wait_ge(loaded[next_k], 16 * next_turn + 16)
                    norm_stats(0, b + 1, x_other)
                if exists(b - 1):
                    h_low(2, b - 1)
                if exists(b + 1):
                    normalise(0, b + 1, x_other)
                if exists(b):
                    dve.wait_ge(zl_hi, b + 1)
                    low(z_l[1][:, :, :], ps_zl, z_l[0][:, :, :]).then_inc(zl_lo, 1)
                if exists(b + 1):
                    h_low(0, b + 1)
                if exists(b):
                    dve.wait_ge(zg_hi, b + 1)
                    low(z_g[1][:, :, :], ps_zg, z_g[0][:, :, :]).then_inc(zg_lo, 1)

            setup()
            steps(dve, body)

        @block.gpsimd
        def _(pool):
            def setup():
                nc.gpsimd.memset(ident[:, :], 0.0).then_inc(setup_ident, 1)
                pool.wait_ge(setup_ident, 1)
                nc.gpsimd.affine_select(out=ident[:, :], in_=ident[:, :], compare_op=ALU.not_equal, fill=1.0,
                                        base=0, pattern=[[-1, P]], channel_multiplier=1).then_inc(setup_ident, 1)
                pool.wait_ge(setup_const, 1)
                pool.wait_ge(setup_load[0], SMALL_LOADS * 16)

            def largest_query(a, e):
                pool.wait_ge(q_maxed[a], e + 1)
                if later(e):
                    pool.wait_ge(row_clamped[a], e)
                    pool.wait_ge(q_subbed[a], e)
                pool.sem_inc(pool_go, 1)
                nc.gpsimd.partition_all_reduce(q_max[:, a:a + 1], q_max1[:, a:a + 1], P, bass.bass_isa.ReduceOp.max).then_inc(q_all[a], 1)

            def e_low(a, e):
                pool.wait_ge(e_hi_01[a], e + 1)
                nc.gpsimd.tensor_tensor(e_hl[a][1][:, 0:2, :], e_full[:, 0:2, :], e_hl[a][0][:, 0:2, :].bitcast(F32),
                                        ALU.subtract).then_inc(e_lo_01[a], 1)

            def sum_first(a, e):
                total = e_sum[:, a, :]
                pool.wait_ge(e_01[a], e + 1)
                if later(e):
                    pool.wait_ge(sums_done[a], e)
                nc.gpsimd.tensor_tensor(total, e_full[:, 0, :], e_full[:, 1, :], ALU.add).then_inc(e_part_sum[a], 1)

            def sum_rest(a, e):
                total = e_sum[:, a, :]
                pool.wait_ge(e_23[a], e + 1)
                pool.wait_ge(e_part_sum[a], 2 * e + 1)
                nc.gpsimd.tensor_tensor(total, total, e_full[:, 2, :], ALU.add).then_inc(e_part_sum[a], 1)
                pool.wait_ge(e_part_sum[a], 2 * e + 2)
                nc.gpsimd.tensor_tensor(total, total, e_full[:, 3, :], ALU.add).then_inc(e_summed[a], 1)

            def deviation(layer, e):
                pool.wait_ge(mean_var_done[layer], e + 1)
                if later(e):
                    pool.wait_ge(rstd_done[layer], e)
                nc.gpsimd.tensor_tensor(var_eps[:, layer, :], mean_var[:, layer, :, 1], eps_col[:, :],
                                        ALU.add).then_inc(var_eps_done[layer], 1)
                pool.wait_ge(var_eps_done[layer], e + 1)
                if later(e):
                    pool.wait_ge(norm_done[layer], e)
                nc.gpsimd.tensor_tensor(rstd[:, layer, :], var_eps[:, layer, :], mhalf_col[:, :],
                                        ALU.pow).then_inc(rstd_done[layer], 1)

            def body(b, k, turn):
                if exists(b - 2):
                    deviation(3, b - 2)
                if exists(b):
                    largest_query(0, b)
                if exists(b - 1):
                    pool.wait_ge(norm_clamped, b)
                    if later(b - 1):
                        pool.wait_ge(degrees, b - 1)
                    nc.gpsimd.tensor_tensor(inv_norm[:, :], norm2[:, :], mhalf_col[:, :], ALU.pow).then_inc(norm_inv, 1)
                if exists(b):
                    sum_first(0, b)
                if exists(b - 2):
                    largest_query(1, b - 2)
                if exists(b):
                    e_low(0, b)
                    sum_rest(0, b)
                if exists(b - 2):
                    sum_first(1, b - 2)
                    e_low(1, b - 2)
                    sum_rest(1, b - 2)
                if exists(b):
                    deviation(1, b)
                if exists(b - 2):
                    pool.wait_ge(o_relu[1], b - 1)
                    nc.gpsimd.tensor_tensor(o_buf[:, 1, :, :], o_buf[:, 1, :, :], x_b[:, k, :, :], ALU.add).then_inc(x4_done, 1)
                if exists(b - 1):
                    deviation(2, b - 1)
                if exists(b + 1):
                    deviation(0, b + 1)
                if exists(b - 1):
                    pool.wait_ge(norm_done[2], b)
                    for t in range(CT):
                        last = nc.gpsimd.tensor_tensor(x_b[:, 1 - k, t, :], x_b[:, 1 - k, t, :], bias_row[:, :], ALU.add)
                    last.then_inc(x_bias, 1)

            setup()
            steps(pool, body)


_INPUTS = ["x", "adj", "L0_gnn_wq", "L0_gnn_wk", "L0_gnn_bm", "L1_gnn_W_lang", "L1_gnn_W_grav", "L1_gnn_W_V",
           "L1_gnn_W_O", "L1_gnn_gate_logit", "L1_gnn_log_sigma", "L2_gnn_bias", "L3_gnn_wq", "L3_gnn_wk", "L3_gnn_bm"]


def kernel(**inputs):
    import numpy as np
    import concourse.bacc as bacc
    from concourse.bass_utils import run_bass_kernel_spmd

    nc = bacc.Bacc("TRN2", target_bir_lowering=False, num_devices=1)
    arrays, args = {}, []
    for name in _INPUTS:
        a = np.ascontiguousarray(inputs[name])
        if a.ndim == 0:
            a = a.reshape(1)
        arrays[f"in_{name}"] = a
        args.append(nc.dram_tensor(f"in_{name}", a.shape, mybir.dt.from_np(a.dtype), kind="ExternalInput").ap())
    out = nc.dram_tensor("out", arrays["in_x"].shape, F32, kind="ExternalOutput").ap()
    emit(nc, *args, out)
    r = run_bass_kernel_spmd(nc, [arrays], core_ids=[0])
    return r.results[0]["out"]
```

```python
from contextlib import ExitStack

import concourse.bass as bass
from concourse import mybir

F32 = mybir.dt.float32
F32R = mybir.dt.float32r
ALU = mybir.AluOpType
ACT = mybir.ActivationFunctionType
AX = mybir.AxisListType

P = 128
LN_EPS = 1e-5
NORM_EPS = 1e-8
SLOPE = 0.01
FIRST_LOOPED = 4
FIRST_LOADS = 5
SMALL_LOADS = 5


def emit(nc, x, adj, wq0, wk0, bm0, w_lang, w_grav, w_v, w_o, gate, log_sigma, bias2, wq3, wk3, bm3, out):
    B, C, N = x.shape
    CT = C // P
    NT = N // P
    D = N
    DT = D // P
    YC = C + 2
    assert B % 2 == 0 and B > FIRST_LOOPED and NT == 4 and CT == 2

    x_view = x.rearrange("b (t p) n -> b p t n", p=P)
    out_view = out.rearrange("b (t p) n -> b p t n", p=P)

    ctx = ExitStack()
    with ctx:
        def sb(name, shape, dt=F32):
            return ctx.enter_context(nc.sbuf_tensor(name, shape, dt))

        def ps(name, shape):
            return ctx.enter_context(nc.psum_tensor(name, shape, F32))

        def split(name, shape):
            return sb(name + "_hi", shape, F32R), sb(name + "_lo", shape, F32R)

        ident = sb("ident", [P, P])
        ones_r = sb("ones_r", [P, P], F32R)
        ones = ones_r[:, :].bitcast(F32)
        wy = split("wy", [P, CT, YC])
        wk_rep = [split(f"wk_rep{a}", [P, CT, P]) for a in range(2)]
        bm_col = sb("bm_col", [P, 2, CT])
        adj_off = sb("adj_off", [P, CT, C])
        w2 = split("w2", [P, CT, C])
        bias_row = sb("bias_row", [P, N])
        lang_t = split("lang_t", [P, DT, D])
        grav_t = split("grav_t", [P, DT, D])
        vo_t = split("vo_t", [P, DT, D])
        scal = sb("scal", [P, 7])
        eps_col = sb("eps_col", [P, CT])
        mhalf_col = sb("mhalf_col", [P, CT])
        neg_inv_var = scal[:, 6:7]
        w_l = scal[:, 5:6]

        x_a = sb("x_a", [P, 2, CT, N])
        x_b = sb("x_b", [P, 2, CT, N])
        norm = sb("norm", [P, CT, N])
        h_a = split("h_a", [P, CT, N])
        h_b = split("h_b", [P, CT, N])
        stats = sb("stats", [P, 4, CT, 6])
        mean_var = sb("mean_var", [P, 4, CT, 2])
        var_eps = sb("var_eps", [P, 4, CT])
        rstd = sb("rstd", [P, 4, CT])
        y = [split(f"y{a}", [P, NT, C]) for a in range(2)]
        q_col = sb("q_col", [P, 2, NT])
        q_max1 = sb("q_max1", [P, 2])
        q_max = sb("q_max", [P, 2])
        q_neg_max = sb("q_neg_max", [P, 2])
        exp_q = sb("exp_q", [P, 2, NT])
        q_slope = sb("q_slope", [P, 2, NT])
        u_row = sb("u_row", [P, N])
        v_row = sb("v_row", [P, N])
        e_full = sb("e_full", [P, NT, N])
        e_sum = sb("e_sum", [P, N])
        e_sum_hl = split("e_sum", [P, N])
        e_hl = [split(f"e{a}", [P, NT, N]) for a in range(2)]
        rec = sb("rec", [P, N])
        o_buf = sb("o_buf", [P, 2, CT, N])
        h_t = split("h_t", [P, DT, C])
        z_l = split("z_l", [P, DT, C])
        z_g = split("z_g", [P, DT, C])
        pv = [t[:, :, :].rearrange("p (n q) c -> p n (q c)", n=CT) for t in z_l]
        k_t = [t[:, 0:CT, :] for t in z_g]
        diag_l = sb("diag_l", [P, CT, P])
        diag_n = diag_l
        diag_g = sb("diag_g", [P, CT, P])
        off_diag = diag_g[:, 0, :]
        lengths = sb("lengths", [P, 4, CT])
        norm2, inv_norm, neg_half_sq, half_sq = [lengths[:, n, :] for n in range(4)]
        mix_l = sb("mix_l", [P, CT, C])
        mix_g = sb("mix_g", [P, CT, C])
        per_row = sb("per_row", [P, 4, 2 * CT])
        degree, degree_inv, coef, weight = [per_row[:, n, :] for n in range(4)]
        w_in = [x_b[:, :, :, :].rearrange("p a t n -> p (a t) n"), e_full[:, :, :],
                o_buf[:, :, :, :].rearrange("p a t n -> p (a t) n")]
        w_v_in = [x_a[:, 1, 0, :], x_a[:, 1, 1, :], mix_l[:, :, :].rearrange("p t c -> p (t c)"),
                  mix_g[:, :, :].rearrange("p t c -> p (t c)")]
        wqk_col, *wqk = [v[:, 0:4 * CT].rearrange("p (a w t) -> p a w t", a=2, w=2)
                         for v in (e_sum, *e_sum_hl)]
        adj_in = u_row[:, :].rearrange("p (t c) -> p t c", t=CT)
        w_o_t = w_in[0]
        w2_full = v_row[:, :].rearrange("p (t c) -> p t c", t=CT)

        ps_a = ps("ps_a", [P, 2, 512])
        ps_b = ps("ps_b", [P, 2, 512])
        ps_c = ps("ps_c", [P, 2, 512])
        ps_6 = ps("ps_6", [P, 512])
        ps_7 = ps("ps_7", [P, 512])
        ps_y = [ps_a, ps_c]
        ps_keys = [ps_7, ps_6]
        ps_sums = ps_6
        ps_o = [ps_c, ps_a]
        ps_zl = ps_a[:, :, :].rearrange("p q (t c) -> p (q t) c", t=2)
        ps_zg = ps_c[:, :, :].rearrange("p q (t c) -> p (q t) c", t=2)
        ps_ht = ps_zg
        gram_l = ps_b[:, 0, :].rearrange("p (t c) -> p t c", t=CT)
        gram_g = ps_b[:, 1, :].rearrange("p (t c) -> p t c", t=CT)
        ps_kt = ps_7[:, :].rearrange("p (t c) -> p t c", t=CT)
        ps_setup = [ps_b, ps_b, ps_a, ps_b, ps_a, ps_b, ps_a, ps_b]

        def half_rows(n):
            return slice(2, 4) if n in (1, 3, 6, 7) else slice(0, 2)

        def diagonal_blocks(bank):
            return bank.rearrange("p (u w) -> p u w", w=P)[:, 0:4:3, :]

        def one(name):
            return ctx.enter_context(nc.semaphore(name))

        def by_attention(name):
            return [one(f"{name}_{a}") for a in range(2)]

        def by_half(name):
            return [one(f"{name}_{n}") for n in range(2)]

        def by_layer(name):
            return [one(f"{name}_{layer}") for layer in range(4)]

        setup_const = one("setup_const")
        setup_ident = one("setup_ident")
        setup_pe = one("setup_pe")
        setup_hi = one("setup_hi")
        setup_lo = one("setup_lo")
        setup_dve = one("setup_dve")
        setup_scal = one("setup_scal")
        stored = one("stored")
        pv_done = by_half("pv_done")
        gram_done = one("gram_done")
        sq_added = one("sq_added")
        norms_spread = one("norms_spread")
        kt_done = one("kt_done")
        kp_done = one("kp_done")
        ht_done = by_half("ht_done")
        zl_done = one("zl_done")
        zg_done = one("zg_done")
        l2_done = one("l2_done")
        diags = one("diags")
        norms2 = one("norms2")
        half_lengths = one("half_lengths")
        norm_clamped = one("norm_clamped")
        norm_inv = one("norm_inv")
        norm_diag = one("norm_diag")
        grav_arg = one("grav_arg")
        grav_exp = one("grav_exp")
        adj_scale = one("adj_scale")
        mixed_l = one("mixed_l")
        mixed_g = one("mixed_g")
        degrees = one("degrees")
        deg_max = one("deg_max")
        deg_inv = one("deg_inv")
        weighted = one("weighted")
        coefs = one("coefs")
        grav_part = one("grav_part")
        k_done = one("k_done")
        kt_hi = one("kt_hi")
        kt_lo = one("kt_lo")
        pv_hi = by_half("pv_hi")
        pv_lo = by_half("pv_lo")
        ht_hi = by_half("ht_hi")
        ht_lo = by_half("ht_lo")
        zl_hi = one("zl_hi")
        zl_lo = one("zl_lo")
        zg_hi = one("zg_hi")
        zg_lo = one("zg_lo")
        x1_done = one("x1_done")
        x2_done = one("x2_done")
        x_bias = one("x_bias")
        x3_done = one("x3_done")
        x4_done = one("x4_done")
        dve_go = one("dve_go")
        pool_go = one("pool_go")
        y_done = by_attention("y_done")
        keys_done = by_attention("keys_done")
        sums_done = by_attention("sums_done")
        o_done = by_attention("o_done")
        q_read = by_attention("q_read")
        q_maxed = by_attention("q_maxed")
        q_all = by_attention("q_all")
        q_shifted = by_attention("q_shifted")
        exp_q_done = by_attention("exp_q_done")
        y_hi_01 = by_attention("y_hi_01")
        y_hi_23 = by_attention("y_hi_23")
        y_lo_01 = by_attention("y_lo_01")
        y_lo = by_attention("y_lo")
        row_clamped = by_attention("row_clamped")
        row_exped = by_attention("row_exped")
        e_v = by_attention("e_v")
        e_01 = by_attention("e_01")
        e_23 = by_attention("e_23")
        e_hi_01 = by_attention("e_hi_01")
        e_hi_23 = by_attention("e_hi_23")
        e_lo_01 = by_attention("e_lo_01")
        e_lo_1 = one("e_lo_1")
        e_lo_23 = by_attention("e_lo_23")
        e_part_sum = by_attention("e_part_sum")
        e_summed = by_attention("e_summed")
        e_sum_hi = by_attention("e_sum_hi")
        e_sum_lo = by_attention("e_sum_lo")
        log_sum = by_attention("log_sum")
        rec_done = by_attention("rec_done")
        o_scaled = by_attention("o_scaled")
        o_relu = by_attention("o_relu")
        stats_done = by_layer("stats_done")
        mean_var_done = by_layer("mean_var_done")
        var_eps_done = by_layer("var_eps_done")
        rstd_done = by_layer("rstd_done")
        norm_done = by_layer("norm_done")
        h_hi = by_layer("h_hi")
        h_lo = by_layer("h_lo")
        loaded = [one(f"loaded_{k}") for k in range(2)]
        setup_load = one("setup_load")
        first_load = one("first_load")
        weight_load = [one(f"weight_load_{n}") for n in range(4)]

        def steps(eng, body):
            for b in range(-1, FIRST_LOOPED):
                body(b, b % 2, b // 2)
            with eng.Fori(FIRST_LOOPED // 2, B // 2 - 1) as turn:
                body(2 * turn, 0, turn)
                body(2 * turn + 1, 1, turn)
            for b in range(B - 2, B + 2):
                body(b, b % 2, b // 2)

        def exists(e):
            return not isinstance(e, int) or 0 <= e < B

        def first(b):
            return isinstance(b, int) and b == 0

        def later(e):
            return not isinstance(e, int) or e > 0

        def other_e_used(eng, a, e, step):
            if a == 1 and exists(e + 2):
                eng.wait_ge(step[0], e + 3)
            elif a == 1 and later(e):
                eng.wait_ge(step[1], e)
            if a == 0 and later(e - 2):
                eng.wait_ge(step[1], e - 2)
            elif a == 0 and later(e):
                eng.wait_ge(step[0], e)

        block = ctx.enter_context(nc.Block())

        @block.sync
        def _(sp):
            sp.dma_start(x_a[:, 0, :, :], x_view[0]).then_inc(loaded[0], 16)
            sp.dma_start(adj_in, adj.rearrange("(t p) c -> p t c", p=P)).then_inc(first_load, 16)
            for a, (wq, wk) in enumerate(((wq0, wk0), (wq3, wk3))):
                for n, w in enumerate((wq, wk)):
                    sp.dma_start(wqk_col[:, a, n, :], w.rearrange("(t p) -> p t", p=P),
                                 allow_slow_non_contiguous=True).then_inc(first_load, 16)
            sp.dma_start(w_in[0], w_lang.rearrange("(t p) d -> p t d", p=P)).then_inc(weight_load[0], 16)
            for a, bm in enumerate((bm0, bm3)):
                sp.dma_start(bm_col[:, a, :], bm.rearrange("(t p) -> p t", p=P),
                             allow_slow_non_contiguous=True).then_inc(setup_load, 16)
            sp.dma_start(scal[:, 0:1], gate.partition_broadcast(P)).then_inc(setup_load, 16)
            sp.dma_start(scal[:, 1:2], log_sigma.partition_broadcast(P)).then_inc(setup_load, 16)
            sp.dma_start(bias_row[:, :], bias2.partition_broadcast(P)).then_inc(setup_load, 16)
            for n, w in ((1, w_o), (2, w_grav)):
                sp.dma_start(w_in[n], w.rearrange("(t p) d -> p t d", p=P)).then_inc(weight_load[n], 16)
            for t in range(DT):
                sp.dma_start(w_v_in[t], w_v[t * P:(t + 1) * P, :]).then_inc(weight_load[3], 16)

            def body(b, k, turn):
                next_k, next_turn = (1, turn) if k == 0 else (0, turn + 1)
                if exists(b) and exists(b + 1):
                    if later(b):
                        sp.wait_ge(x2_done, b)
                    else:
                        sp.wait_ge(setup_pe, 9)
                    sp.dma_start(x_a[:, next_k, :, :], x_view[b + 1]).then_inc(loaded[next_k], 16)
                if exists(b - 2):
                    sp.wait_ge(x4_done, b - 1)
                    sp.dma_start(out_view[b - 2], o_buf[:, 1, :, :]).then_inc(stored, 16)

            steps(sp, body)
            sp.wait_ge(stored, 16 * B)

        @block.tensor
        def _(pe):
            def passes(out, left, right, start, stop):
                nc.tensor.matmul(out, left[0], right[0], start=start, stop=False, skip_group_check=True)
                nc.tensor.matmul(out, left[0], right[1], start=False, stop=False, skip_group_check=True)
                return nc.tensor.matmul(out, left[1], right[0], start=False, stop=stop, skip_group_check=True)

            def setup():
                pe.wait_ge(first_load, FIRST_LOADS * 16)
                pe.wait_ge(setup_ident, 2)
                for t in range(CT):
                    for o in range(CT):
                        last = nc.tensor.transpose(ps_6[:, t * C + o * P:t * C + (o + 1) * P],
                                                   adj_in[:, o, t * P:(t + 1) * P], ident[:, :])
                last.then_inc(setup_pe, 1)

            def turn_weight(n, w, half, load):
                pe.wait_ge(load, 16)
                if n == 2:
                    pe.wait_ge(y_lo[0], 1)
                elif n in (1, 3):
                    pe.wait_ge(setup_lo, (n + 3) // 2)
                elif n == 5:
                    pe.wait_ge(setup_hi, 5)
                elif n == 6:
                    pe.wait_ge(setup_lo, 4)
                for q in range(2):
                    for t in range(DT):
                        c = (2 * half + q) * P
                        last = nc.tensor.transpose(ps_setup[n][:, q, t * P:(t + 1) * P], w[:, t, c:c + P],
                                                   ident[:, :])
                last.then_inc(setup_pe, 1)

            def weight_product(n, half):
                pe.wait_ge(weight_load[3], DT * 16)
                pe.wait_ge(setup_hi, 5)
                if n == 7:
                    pe.wait_ge(setup_lo, 5)
                for q in range(2):
                    c = (2 * half + q) * P
                    for t in range(DT):
                        last = nc.tensor.matmul(ps_setup[n][:, q, :], w_v_in[t][:, c:c + P], w_o_t[:, t, :],
                                                start=(t == 0), stop=(t == DT - 1))
                last.then_inc(setup_pe, 1)

            def project(a, e):
                h = (h_a, h_b)[a]
                pe.wait_ge(h_hi[(0, 3)[a]], e + 1)
                if a == 0 and first(e):
                    pe.wait_ge(setup_lo, 1)
                if a == 0 and later(e):
                    pe.wait_ge(zl_lo, e)
                if a == 1 and exists(e + 2):
                    pe.wait_ge(y_lo[0], e + 3)
                elif a == 1 and exists(e + 1):
                    pe.wait_ge(zg_lo, e + 2)
                elif a == 1:
                    pe.wait_ge(o_scaled[1], e)
                for n in range(NT):
                    if a == 0 and n == 2 and later(e):
                        pe.wait_ge(zg_lo, e)
                    for t in range(CT):
                        for w in wy:
                            nc.tensor.matmul(ps_y[n // 2][:, n % 2, 0:YC], h[0][:, t, n * P:(n + 1) * P], w[:, t, :],
                                             start=(t == 0 and w is wy[0]), stop=False, skip_group_check=True)
                pe.wait_ge(h_lo[(0, 3)[a]], e + 1)
                for n in range(NT):
                    for t in range(CT):
                        last = nc.tensor.matmul(ps_y[n // 2][:, n % 2, 0:YC], h[1][:, t, n * P:(n + 1) * P],
                                                wy[0][:, t, :], start=False, stop=(t == CT - 1), skip_group_check=True)
                last.then_inc(y_done[a], 1)
                if a == 0 and first(e):
                    pe.wait_ge(setup_ident, 3)
                if a == 0 and later(e - 1):
                    pe.wait_ge(kt_lo, e - 1)
                if a == 1 and later(e):
                    pe.wait_ge(log_sum[1], e)
                for t in range(CT):
                    last = passes(ps_keys[a][:, :], [w[:, t, :] for w in wk_rep[a]], [x[:, t, :] for x in h],
                                  t == 0, t == CT - 1)
                last.then_inc(keys_done[a], 1)

            def attend(a, e):
                pe.wait_ge(y_lo[a], e + 1)
                if a == 0 and later(e - 1):
                    pe.wait_ge(y_lo[1], e - 1)
                for o, half in ((0, 0), (1, 0), (0, 1), (1, 1)):
                    pe.wait_ge((e_lo_01, e_lo_23)[half][a], e + 1)
                    if a == 0 and half == 0:
                        pe.wait_ge(e_lo_1, e + 1)
                    if a == 1 and half == 0 and exists(e + 1):
                        pe.wait_ge(pv_lo[o], e + 2)
                    for n in (2 * half, 2 * half + 1):
                        last = passes(ps_o[a][:, o, :], [v[:, n, o * P:(o + 1) * P] for v in y[a]],
                                      [v[:, n, :] for v in e_hl[a]], n == 0, n == NT - 1)
                last.then_inc(o_done[a], 1)
                pe.wait_ge(e_sum_lo[a], e + 1)
                if a == 0 and later(e - 1):
                    pe.wait_ge(row_clamped[1], e - 1)
                elif a == 0 and later(e):
                    pe.wait_ge(log_sum[0], e)
                if a == 1 and exists(e + 2):
                    pe.wait_ge(log_sum[0], e + 3)
                nc.tensor.matmul(ps_sums[:, :], ones_r[:, :], e_sum_hl[0][:, :], start=True, stop=False)
                nc.tensor.matmul(ps_sums[:, :], ones_r[:, :], e_sum_hl[1][:, :], start=False,
                                 stop=True).then_inc(sums_done[a], 1)

            def grams(e):
                pe.wait_ge(zg_lo, e + 1)
                if later(e):
                    pe.wait_ge(x3_done, e)
                else:
                    pe.wait_ge(setup_lo, 7)
                for gram, z in ((gram_l, z_l), (gram_g, z_g)):
                    for n in range(CT):
                        for t in range(DT):
                            last = passes(gram[:, n, :], [v[:, t, n * P:(n + 1) * P] for v in z],
                                          [v[:, t, :] for v in z], n == 0 and t == 0, t == DT - 1)
                last.then_inc(gram_done, 1)

            def add_lengths(e):
                pe.wait_ge(diags, e + 1)
                for n in range(CT):
                    last = nc.tensor.matmul(gram_g[:, n, :], ones, diag_g[:, :, :].rearrange("p t c -> p (t c)"),
                                            start=False, stop=True, skip_group_check=True)
                last.then_inc(sq_added, 1)

            def spread_norms(e):
                pe.wait_ge(norm_diag, e + 1)
                if exists(e + 1):
                    pe.wait_ge(row_clamped[0], e + 2)
                elif later(e):
                    pe.wait_ge(kt_lo, e)
                nc.tensor.matmul(ps_7[:, 0:C], ones, diag_n[:, :, :].rearrange("p t c -> p (t c)"),
                                 start=True, stop=True).then_inc(norms_spread, 1)

            def values(n, e):
                if n == 0 and later(e):
                    pe.wait_ge(y_lo_01[1], e)
                elif n == 0 and exists(e + 1):
                    pe.wait_ge(y_lo[0], e + 2)
                for t in range(DT):
                    last = passes(ps_a[:, n, :], [v[:, t, n * P:(n + 1) * P] for v in h_t],
                                  [w[:, t, :] for w in vo_t], t == 0, t == DT - 1)
                last.then_inc(pv_done[n], 1)

            def turn_mixing(e):
                pe.wait_ge(k_done, e + 1)
                for t in range(CT):
                    for n in range(CT):
                        last = nc.tensor.transpose(ps_kt[:, t, n * P:(n + 1) * P], mix_l[:, n, t * P:(t + 1) * P],
                                                   ident[:, :])
                last.then_inc(kt_done, 1)

            def mix(parts, e):
                pe.wait_ge(kt_lo, e + 1)
                pe.wait_ge(pv_lo[1], e + 1)
                for n, t in parts:
                    last = passes(ps_b[:, n, :], [v[:, t, n * P:(n + 1) * P] for v in k_t],
                                  [v[:, t, :] for v in pv], t == 0, t == CT - 1)
                if parts[-1] == (1, 1):
                    last.then_inc(kp_done, 1)

            def turn_h(e):
                pe.wait_ge(norm_done[1], e + 1)
                for t in range(DT):
                    for n in range(CT):
                        last = nc.tensor.transpose(ps_ht[:, t, n * P:(n + 1) * P], norm[:, n, t * P:(t + 1) * P],
                                                   ident[:, :])
                    if t % 2 == 1:
                        last.then_inc(ht_done[t // 2], 1)

            def fixed(e):
                pe.wait_ge(h_hi[2], e + 1)
                for m in range(CT):
                    for n in range(CT):
                        for w in w2:
                            nc.tensor.matmul(ps_b[:, m, :], w[:, n, m * P:(m + 1) * P], h_b[0][:, n, :],
                                             start=(n == 0 and w is w2[0]), stop=False, skip_group_check=True)
                pe.wait_ge(h_lo[2], e + 1)
                for m in range(CT):
                    for n in range(CT):
                        last = nc.tensor.matmul(ps_b[:, m, :], w2[0][:, n, m * P:(m + 1) * P], h_b[1][:, n, :],
                                                start=False, stop=(n == CT - 1), skip_group_check=True)
                last.then_inc(l2_done, 1)

            def z_of(target, weight_t, e, done):
                for o in range(DT):
                    parts = [w[:, :, o * P:(o + 1) * P] for w in weight_t]
                    for t in range(DT):
                        if o == 0 and t % 2 == 0:
                            pe.wait_ge(ht_hi[t // 2], e + 1)
                        for part in parts:
                            nc.tensor.matmul(target[:, o, :], part[:, t, :], h_t[0][:, t, :],
                                             start=(o % 2 == 0 and t == 0 and part is parts[0]), stop=False,
                                             skip_group_check=True)
                    for t in range(DT):
                        if o == 0 and t % 2 == 0:
                            pe.wait_ge(ht_lo[t // 2], e + 1)
                        last = nc.tensor.matmul(target[:, o, :], parts[0][:, t, :], h_t[1][:, t, :], start=False,
                                                stop=(t == DT - 1), skip_group_check=True)
                last.then_inc(done, 1)

            def body(b, k, turn):
                if exists(b):
                    project(0, b)
                if first(b):
                    turn_weight(1, w_in[0], 1, weight_load[0])
                    for half in range(2):
                        turn_weight(2 + half, w_in[1], half, weight_load[1])
                    weight_product(4, 0)
                    for half in range(2):
                        turn_weight(5 + half, w_in[2], half, weight_load[2])
                if exists(b - 1):
                    grams(b - 1)
                if exists(b - 2):
                    project(1, b - 2)
                if exists(b - 1):
                    add_lengths(b - 1)
                    spread_norms(b - 1)
                    values(0, b - 1)
                if exists(b):
                    attend(0, b)
                if first(b):
                    weight_product(7, 1)
                if exists(b - 1):
                    values(1, b - 1)
                    turn_mixing(b - 1)
                if exists(b - 1) and not exists(b):
                    mix(((0, 0), (0, 1), (1, 0), (1, 1)), b - 1)
                if exists(b - 2):
                    attend(1, b - 2)
                if exists(b - 1) and exists(b):
                    mix(((0, 0), (0, 1), (1, 0)), b - 1)
                if exists(b):
                    turn_h(b)
                if exists(b - 1) and exists(b):
                    mix(((1, 1),), b - 1)
                if exists(b):
                    if first(b):
                        pe.wait_ge(setup_lo, 6)
                    if later(b - 1):
                        pe.wait_ge(o_scaled[1], b - 1)
                    elif later(b):
                        pe.wait_ge(pv_lo[1], b)
                    z_of(ps_zl, lang_t, b, zl_done)
                    z_of(ps_zg, grav_t, b, zg_done)
                if exists(b - 1):
                    fixed(b - 1)

            setup()
            turn_weight(0, w_in[0], 0, weight_load[0])
            steps(pe, body)

        @block.scalar
        def _(act):
            def setup():
                act.wait_ge(setup_load, SMALL_LOADS * 16)
                nc.scalar.activation(scal[:, 2:3], scal[:, 1:2], ACT.Exp, scale=-2.0)
                nc.scalar.activation(scal[:, 3:4], scal[:, 0:1], ACT.Exp, scale=-1.0).then_inc(setup_scal, 1)

            def first_operands():
                act.wait_ge(first_load, FIRST_LOADS * 16)
                nc.scalar.copy(wqk[0], wqk_col).then_inc(setup_scal, 1)
                act.wait_ge(setup_pe, 1)
                nc.scalar.copy(wy[0][:, :, 0:C], ps_6[:, :].rearrange("p (t c) -> p t c", t=CT)).then_inc(setup_hi, 1)

            def weight_high(n):
                act.wait_ge(setup_pe, n + 2)
                target = ((lang_t[0], w_o_t)[n // 2] if n < 4 else vo_t[0] if n in (4, 7) else grav_t[0])
                nc.scalar.copy(target[:, half_rows(n), :], ps_setup[n][:, :, :]).then_inc(setup_hi, 1)

            def y_high(a, e):
                act.wait_ge(y_done[a], e + 1)
                if later(e):
                    act.wait_ge(q_shifted[a], e)
                    act.wait_ge(exp_q_done[a], e)
                    act.wait_ge(o_done[a], e)
                for g in range(2):
                    last = nc.scalar.copy(q_col[:, a, 2 * g:2 * g + 2], ps_y[g][:, :, C + a])
                last.then_inc(q_read[a], 1)
                nc.scalar.copy(y[a][0][:, 0:2, :], ps_y[0][:, :, 0:C]).then_inc(y_hi_01[a], 1)
                nc.scalar.copy(y[a][0][:, 2:4, :], ps_y[1][:, :, 0:C]).then_inc(y_hi_23[a], 1)

            def exponentials(a, e):
                act.wait_ge(q_shifted[a], e + 1)
                if later(e):
                    act.wait_ge(e_23[a], e)
                nc.scalar.activation(exp_q[:, a, :], q_col[:, a, :], ACT.Exp, bias=q_neg_max[:, a:a + 1]).then_inc(exp_q_done[a], 1)
                act.wait_ge(keys_done[a], e + 1)
                other_e_used(act, a, e, e_23)
                nc.scalar.activation(u_row[:, :], ps_keys[a][:, :], ACT.Relu, bias=q_neg_max[:, a:a + 1], scale=-1.0)
                nc.scalar.activation(v_row[:, :], ps_keys[a][:, :], ACT.Relu,
                                     bias=q_max[:, a:a + 1]).then_inc(row_clamped[a], 1)
                act.wait_ge(row_clamped[a], e + 1)
                nc.scalar.activation(u_row[:, :], u_row[:, :], ACT.Exp, scale=SLOPE - 1.0).then_inc(row_exped[a], 1)

            def slope_exponentials(a, e):
                other_e_used(act, a, e, e_summed)
                other_e_used(act, a, e, e_lo_01)
                other_e_used(act, a, e, e_lo_23)
                for n in range(NT):
                    nc.scalar.activation(e_full[:, n, :], v_row[:, :], ACT.Exp, bias=q_slope[:, a, n:n + 1],
                                         scale=SLOPE - 1.0).then_inc(e_v[a], 1)

            def value_high(n, e):
                act.wait_ge(pv_done[n], e + 1)
                nc.scalar.copy(pv[0][:, n, :], ps_a[:, n, :]).then_inc(pv_hi[n], 1)

            def e_high_01(a, e):
                act.wait_ge(e_01[a], e + 1)
                nc.scalar.copy(e_hl[a][0][:, 0:2, :], e_full[:, 0:2, :]).then_inc(e_hi_01[a], 1)

            def e_high_23(a, e):
                act.wait_ge(e_23[a], e + 1)
                nc.scalar.copy(e_hl[a][0][:, 2:4, :], e_full[:, 2:4, :]).then_inc(e_hi_23[a], 1)

            def sum_high(a, e):
                act.wait_ge(e_summed[a], e + 1)
                other_e_used(act, a, e, sums_done)
                nc.scalar.copy(e_sum_hl[0][:, :], e_sum[:, :]).then_inc(e_sum_hi[a], 1)

            def gravity(e):
                act.wait_ge(sq_added, e + 1)
                act.wait_ge(half_lengths, e + 1)
                if later(e):
                    act.wait_ge(k_done, e)
                for n in range(CT):
                    last = nc.scalar.activation(mix_g[:, n, :], gram_g[:, n, :], ACT.Relu, bias=half_sq[:, n:n + 1],
                                                scale=-1.0)
                last.then_inc(grav_arg, 1)
                act.wait_ge(grav_arg, e + 1)
                nc.scalar.activation(mix_g[:, :, :], mix_g[:, :, :], ACT.Exp, scale=neg_inv_var).then_inc(grav_exp, 1)

            def inverse_sums(a, e):
                act.wait_ge(sums_done[a], e + 1)
                if a == 0 and later(e - 2):
                    act.wait_ge(o_scaled[1], e - 2)
                elif a == 0 and later(e):
                    act.wait_ge(o_scaled[0], e)
                if a == 1 and exists(e + 2):
                    act.wait_ge(o_scaled[0], e + 3)
                elif a == 1 and later(e):
                    act.wait_ge(o_scaled[1], e)
                nc.scalar.activation(rec[:, :], ps_sums[:, :], ACT.Ln).then_inc(log_sum[a], 1)
                act.wait_ge(log_sum[a], e + 1)
                nc.scalar.activation(rec[:, :], rec[:, :], ACT.Exp, scale=-1.0).then_inc(rec_done[a], 1)

            def biased_relu(a, e):
                act.wait_ge(o_scaled[a], e + 1)
                for o in range(CT):
                    last = nc.scalar.activation(o_buf[:, a, o, :], o_buf[:, a, o, :], ACT.Relu,
                                                bias=bm_col[:, a, o:o + 1])
                last.then_inc(o_relu[a], 1)

            def h_high(layer, e):
                act.wait_ge(norm_done[layer], e + 1)
                if layer == 0 and later(e):
                    act.wait_ge(keys_done[0], e)
                if layer == 2 and later(e):
                    act.wait_ge(keys_done[1], e)
                if layer == 3:
                    act.wait_ge(l2_done, e + 1)
                h = h_a if layer == 0 else h_b
                nc.scalar.activation(h[0][:, :, :], norm[:, :, :], ACT.Relu).then_inc(h_hi[layer], 1)

            def body(b, k, turn):
                if first(b):
                    setup()
                    weight_high(0)
                if exists(b):
                    y_high(0, b)
                if first(b):
                    weight_high(1)
                    weight_high(2)
                if exists(b - 2):
                    h_high(3, b - 2)
                if exists(b):
                    exponentials(0, b)
                if first(b):
                    weight_high(3)
                if exists(b):
                    slope_exponentials(0, b)
                if exists(b - 2):
                    y_high(1, b - 2)
                if exists(b):
                    e_high_01(0, b)
                if exists(b - 1):
                    gravity(b - 1)
                if exists(b):
                    e_high_23(0, b)
                if first(b):
                    weight_high(4)
                    weight_high(5)
                    weight_high(6)
                if exists(b - 2):
                    exponentials(1, b - 2)
                if exists(b):
                    sum_high(0, b)
                if exists(b - 2):
                    slope_exponentials(1, b - 2)
                    e_high_01(1, b - 2)
                if exists(b - 1):
                    value_high(0, b - 1)
                if exists(b):
                    inverse_sums(0, b)
                if exists(b - 1):
                    value_high(1, b - 1)
                if exists(b - 2):
                    e_high_23(1, b - 2)
                if exists(b):
                    biased_relu(0, b)
                if first(b):
                    weight_high(7)
                if exists(b - 1):
                    act.wait_ge(kt_done, b)
                    nc.scalar.copy(k_t[0], ps_kt).then_inc(kt_hi, 1)
                if exists(b - 2):
                    sum_high(1, b - 2)
                if exists(b - 1) and not exists(b):
                    h_high(2, b - 1)
                if exists(b - 2):
                    inverse_sums(1, b - 2)
                if exists(b):
                    if later(b):
                        act.wait_ge(pv_done[1], b)
                    for half in range(2):
                        rows = slice(2 * half, 2 * half + 2)
                        act.wait_ge(ht_done[half], b + 1)
                        nc.scalar.activation(h_t[0][:, rows, :], ps_ht[:, rows, :], ACT.Relu).then_inc(ht_hi[half], 1)
                if exists(b - 2):
                    biased_relu(1, b - 2)
                if exists(b - 1) and exists(b):
                    h_high(2, b - 1)
                if exists(b):
                    act.wait_ge(zl_done, b + 1)
                    if later(b):
                        act.wait_ge(kp_done, b)
                    nc.scalar.copy(z_l[0][:, :, :], ps_zl).then_inc(zl_hi, 1)
                if exists(b + 1):
                    h_high(0, b + 1)
                if exists(b):
                    act.wait_ge(zg_done, b + 1)
                    nc.scalar.copy(z_g[0][:, :, :], ps_zg).then_inc(zg_hi, 1)

            nc.scalar.preload_act_table_set("natural_log_exp_and_others")
            first_operands()
            steps(act, body)

        @block.vector
        def _(dve):
            def low(out_lo, full, hi):
                return nc.vector.tensor_tensor(out_lo, full, hi.bitcast(F32), ALU.subtract)

            def constants():
                nc.vector.memset(eps_col[:, :], LN_EPS)
                nc.vector.memset(mhalf_col[:, :], -0.5)
                nc.vector.memset(diag_g[:, 0, :], 1.0).then_inc(setup_const, 1)
                dve.wait_ge(setup_const, 1)
                nc.vector.tensor_copy(ones_r[:, :], diag_g[:, 0, :]).then_inc(setup_const, 1)

            def first_operands():
                dve.wait_ge(setup_scal, 1)
                low(wqk[1], wqk_col, wqk[0]).then_inc(setup_dve, 1)
                dve.wait_ge(setup_dve, 1)
                for a in range(2):
                    for half in range(2):
                        for t in range(CT):
                            nc.vector.tensor_copy(wy[half][:, t, C + a:C + a + 1],
                                                  wqk[half][:, a, 0, t:t + 1].bitcast(F32))
                dve.wait_ge(setup_hi, 1)
                low(wy[1][:, :, 0:C], ps_6[:, :].rearrange("p (t c) -> p t c", t=CT), wy[0][:, :, 0:C]).then_inc(setup_lo, 1)

            def setup():
                dve.wait_ge(setup_ident, 2)
                nc.vector.tensor_scalar(off_diag, ident[:, :], -1.0, 1.0, ALU.mult, ALU.add)
                dve.wait_ge(setup_scal, 2)
                nc.vector.tensor_scalar(neg_inv_var, scal[:, 2:3], -1.0, None, ALU.mult)
                nc.vector.tensor_scalar_add(scal[:, 4:5], scal[:, 3:4], 1.0).then_inc(setup_dve, 1)
                dve.wait_ge(setup_dve, 2)
                nc.vector.reciprocal(scal[:, 5:6], scal[:, 4:5])
                nc.vector.tensor_tensor(w2_full[:, :, :], adj_in, adj_in, ALU.mult)
                for t in range(CT):
                    for c in range(CT):
                        block_of = lambda m: m[:, t, c * P:(c + 1) * P]
                        if t == c:
                            last = nc.vector.tensor_tensor(block_of(adj_off), block_of(adj_in), off_diag, ALU.mult)
                        else:
                            last = nc.vector.tensor_copy(block_of(adj_off), block_of(adj_in))
                last.then_inc(setup_dve, 1)
                dve.wait_ge(setup_dve, 3)
                nc.vector.tensor_scalar(weight[:, CT:2 * CT], w_l.to_broadcast([P, CT]), -1.0, 1.0, ALU.mult, ALU.add)
                nc.vector.tensor_copy(w2[0][:, :, :], w2_full[:, :, :]).then_inc(setup_dve, 1)
                dve.wait_ge(setup_dve, 4)
                low(w2[1][:, :, :], w2_full[:, :, :], w2[0][:, :, :])

            def weight_low(n):
                dve.wait_ge(setup_hi, n + 2)
                target, rows = lang_t if n < 2 else vo_t if n in (4, 7) else grav_t, half_rows(n)
                low(target[1][:, rows, :], ps_setup[n][:, :, :], target[0][:, rows, :]).then_inc(setup_lo, 1)

            def norm_stats(layer, e, x_in):
                for t in range(CT):
                    last = nc.vector.bn_stats(stats[:, layer, t, :], x_in[:, t, :])
                last.then_inc(stats_done[layer], 1)
                dve.wait_ge(stats_done[layer], e + 1)
                if later(e):
                    dve.wait_ge(norm_done[layer], e)
                dve.sem_inc(dve_go, 1)
                for t in range(CT):
                    last = nc.vector.bn_aggr(mean_var[:, layer, t, :], stats[:, layer, t, :])
                last.then_inc(mean_var_done[layer], 1)

            def normalise(layer, e, x_in):
                dve.wait_ge(rstd_done[layer], e + 1)
                if layer == 3 and exists(e + 2):
                    dve.wait_ge(h_lo[0], e + 3)
                elif layer == 3:
                    dve.wait_ge(h_lo[2], e + 1)
                if layer == 1 and later(e - 1):
                    dve.wait_ge(h_lo[3], e - 1)
                elif layer == 1:
                    dve.wait_ge(h_lo[0], e + 1)
                if layer == 2 and exists(e + 1):
                    dve.wait_ge(ht_done[1], e + 2)
                elif layer == 2:
                    dve.wait_ge(h_lo[3], e)
                if layer == 0 and later(e - 1):
                    dve.wait_ge(h_lo[2], e - 1)
                elif layer == 0 and later(e):
                    dve.wait_ge(h_lo[0], e)
                for t in range(CT):
                    last = nc.vector.tensor_scalar(norm[:, t, :], x_in[:, t, :], mean_var[:, layer, t, 0:1],
                                                   rstd[:, layer, t:t + 1], ALU.subtract, ALU.mult)
                last.then_inc(norm_done[layer], 1)

            def h_low(layer, e):
                dve.wait_ge(h_hi[layer], e + 1)
                h = h_a if layer == 0 else h_b
                nc.vector.scalar_tensor_tensor(h[1][:, :, :].rearrange("p t n -> p (t n)"),
                                               norm[:, :, :].rearrange("p t n -> p (t n)"), 0.0,
                                               h[0][:, :, :].bitcast(F32).rearrange("p t n -> p (t n)"),
                                               ALU.max, ALU.subtract).then_inc(h_lo[layer], 1)

            def queries(a, e):
                dve.wait_ge(q_read[a], e + 1)
                if later(e):
                    dve.wait_ge(q_all[a], e)
                nc.vector.reduce_max(q_max1[:, a:a + 1], q_col[:, a, :], axis=AX.X).then_inc(q_maxed[a], 1)

            def y_low(a, e):
                dve.wait_ge(y_hi_01[a], e + 1)
                low(y[a][1][:, 0:2, :], ps_y[0][:, :, 0:C], y[a][0][:, 0:2, :]).then_inc(y_lo_01[a], 1)
                dve.wait_ge(y_hi_23[a], e + 1)
                low(y[a][1][:, 2:4, :], ps_y[1][:, :, 0:C], y[a][0][:, 2:4, :]).then_inc(y_lo[a], 1)

            def shift_queries(a, e):
                dve.wait_ge(q_all[a], e + 1)
                if later(e):
                    dve.wait_ge(exp_q_done[a], e)
                    dve.wait_ge(row_clamped[a], e)
                    dve.wait_ge(e_v[a], NT * e)
                nc.vector.tensor_scalar(q_neg_max[:, a:a + 1], q_max[:, a:a + 1], -1.0, None, ALU.mult)
                nc.vector.tensor_scalar(q_slope[:, a, :], q_col[:, a, :], q_max[:, a:a + 1], SLOPE, ALU.subtract,
                                        ALU.mult).then_inc(q_shifted[a], 1)

            def numerators(n, a, e):
                if n == 0:
                    dve.wait_ge(exp_q_done[a], e + 1)
                    dve.wait_ge(row_exped[a], e + 1)
                dve.wait_ge(e_v[a], NT * e + n + 1)
                done = nc.vector.scalar_tensor_tensor(e_full[:, n, :], u_row[:, :], exp_q[:, a, n:n + 1],
                                                      e_full[:, n, :], ALU.mult, ALU.max)
                if n == 1:
                    done.then_inc(e_01[a], 1)
                if n == 3:
                    done.then_inc(e_23[a], 1)

            def e_low(a, e):
                if a == 0:
                    dve.wait_ge(e_hi_01[0], e + 1)
                    low(e_hl[0][1][:, 1, :], e_full[:, 1, :], e_hl[0][0][:, 1, :]).then_inc(e_lo_1, 1)
                dve.wait_ge(e_hi_23[a], e + 1)
                low(e_hl[a][1][:, 2:4, :], e_full[:, 2:4, :], e_hl[a][0][:, 2:4, :]).then_inc(e_lo_23[a], 1)

            def value_low(n, e):
                dve.wait_ge(pv_hi[n], e + 1)
                low(pv[1][:, n, :], ps_a[:, n, :], pv[0][:, n, :]).then_inc(pv_lo[n], 1)

            def gram_diagonals(e):
                dve.wait_ge(gram_done, e + 1)
                if later(e):
                    dve.wait_ge(sq_added, e)
                    dve.wait_ge(norms_spread, e)
                eye = ident[:, :].unsqueeze(1).to_broadcast([P, CT, P])
                nc.vector.tensor_tensor(diag_l[:, :, :], diagonal_blocks(ps_b[:, 0, :]), eye, ALU.mult)
                nc.vector.scalar_tensor_tensor(diag_g[:, :, :], diagonal_blocks(ps_b[:, 1, :]), -0.5, eye,
                                               ALU.mult, ALU.mult).then_inc(diags, 1)
                dve.wait_ge(diags, e + 1)
                nc.vector.reduce_sum(norm2, diag_l[:, :, :], axis=AX.X)
                nc.vector.reduce_sum(neg_half_sq, diag_g[:, :, :], axis=AX.X).then_inc(norms2, 1)
                dve.wait_ge(norms2, e + 1)
                if later(e):
                    dve.wait_ge(grav_arg, e)
                nc.vector.tensor_scalar(half_sq, neg_half_sq, -1.0, None, ALU.mult).then_inc(half_lengths, 1)
                nc.vector.tensor_scalar_max(norm2, norm2, NORM_EPS * NORM_EPS).then_inc(norm_clamped, 1)

            def inverse_norms(e):
                dve.wait_ge(norm_inv, e + 1)
                dve.wait_ge(norms2, e + 1)
                for t in range(CT):
                    last = nc.vector.tensor_scalar(diag_n[:, t, :], ident[:, :], inv_norm[:, t:t + 1], None, ALU.mult)
                last.then_inc(norm_diag, 1)
                if later(e):
                    dve.wait_ge(coefs, e)
                nc.vector.tensor_scalar(weight[:, 0:CT], inv_norm, w_l, None, ALU.mult).then_inc(weighted, 1)

            def mixing_kernels(e):
                dve.wait_ge(norms_spread, e + 1)
                if later(e):
                    dve.wait_ge(kt_done, e)
                nc.vector.tensor_tensor(mix_l[:, :, :], adj_off[:, :, :],
                                        ps_7[:, 0:C].unsqueeze(1).to_broadcast([P, CT, C]), ALU.mult).then_inc(adj_scale, 1)
                dve.wait_ge(adj_scale, e + 1)
                if later(e):
                    dve.wait_ge(deg_inv, e)
                for n in range(CT):
                    last = nc.vector.scalar_tensor_tensor(mix_l[:, n, :], gram_l[:, n, :], 0.0, mix_l[:, n, :],
                                                          ALU.max, ALU.mult, accum_out=degree[:, n:n + 1])
                last.then_inc(mixed_l, 1)
                dve.wait_ge(grav_exp, e + 1)
                for n in range(CT):
                    last = nc.vector.scalar_tensor_tensor(mix_g[:, n, :], mix_g[:, n, :], 1.0, adj_off[:, n, :],
                                                          ALU.mult, ALU.mult, accum_out=degree[:, CT + n:CT + n + 1])
                last.then_inc(mixed_g, 1)

            def scale_row_sums(e):
                dve.wait_ge(mixed_g, e + 1)
                nc.vector.tensor_tensor(degree[:, 0:CT], degree[:, 0:CT], inv_norm, ALU.mult).then_inc(degrees, 1)

            def clamp_row_sums(e):
                dve.wait_ge(degrees, e + 1)
                nc.vector.tensor_scalar_max(degree, degree, NORM_EPS).then_inc(deg_max, 1)

            def invert_row_sums(e):
                dve.wait_ge(deg_max, e + 1)
                nc.vector.reciprocal(degree_inv, degree).then_inc(deg_inv, 1)

            def coefficients(e):
                dve.wait_ge(deg_inv, e + 1)
                nc.vector.tensor_tensor(coef, degree_inv, weight, ALU.mult).then_inc(coefs, 1)

            def scale_gravity(e):
                dve.wait_ge(coefs, e + 1)
                for n in range(CT):
                    last = nc.vector.tensor_scalar(mix_g[:, n, :], mix_g[:, n, :], coef[:, CT + n:CT + n + 1], None, ALU.mult)
                last.then_inc(grav_part, 1)

            def mixing_sum(e):
                dve.wait_ge(grav_part, e + 1)
                for n in range(CT):
                    last = nc.vector.scalar_tensor_tensor(mix_l[:, n, :], mix_l[:, n, :], coef[:, n:n + 1],
                                                          mix_g[:, n, :], ALU.mult, ALU.add)
                last.then_inc(k_done, 1)

            def scale_out(a, e):
                dve.wait_ge(rec_done[a], e + 1)
                dve.wait_ge(o_done[a], e + 1)
                if a == 0 and later(e):
                    dve.wait_ge(x1_done, e)
                if a == 1 and later(e):
                    dve.wait_ge(stored, 16 * e)
                nc.vector.tensor_tensor(o_buf[:, a, :, :], ps_o[a][:, :, :],
                                        rec[:, :].unsqueeze(1).to_broadcast([P, CT, N]), ALU.mult).then_inc(o_scaled[a], 1)

            def body(b, k, turn):
                x_now, x_other = x_a[:, k, :, :], x_a[:, 1 - k, :, :]
                x_b_old, x_b_last = x_b[:, k, :, :], x_b[:, 1 - k, :, :]
                if first(b):
                    weight_low(0)
                    setup()
                if exists(b - 2):
                    dve.wait_ge(l2_done, b - 1)
                    dve.wait_ge(x_bias, b - 1)
                    nc.vector.tensor_tensor(x_b_old, x_b_old, ps_b[:, :, :], ALU.add).then_inc(x3_done, 1)
                    dve.wait_ge(x3_done, b - 1)
                    norm_stats(3, b - 2, x_b_old)
                if exists(b):
                    queries(0, b)
                if exists(b - 2):
                    normalise(3, b - 2, x_b_old)
                if exists(b):
                    y_low(0, b)
                if first(b):
                    weight_low(1)
                if exists(b - 2):
                    h_low(3, b - 2)
                if exists(b):
                    shift_queries(0, b)
                if exists(b - 1):
                    gram_diagonals(b - 1)
                if exists(b):
                    numerators(0, 0, b)
                    numerators(1, 0, b)
                if exists(b - 1):
                    inverse_norms(b - 1)
                if exists(b - 2):
                    queries(1, b - 2)
                    y_low(1, b - 2)
                if exists(b):
                    numerators(2, 0, b)
                    numerators(3, 0, b)
                if exists(b - 2):
                    shift_queries(1, b - 2)
                if exists(b):
                    e_low(0, b)
                if first(b):
                    weight_low(4)
                    weight_low(5)
                    weight_low(6)
                if exists(b - 1):
                    mixing_kernels(b - 1)
                if exists(b - 2):
                    numerators(0, 1, b - 2)
                if exists(b - 1):
                    scale_row_sums(b - 1)
                if exists(b - 2):
                    numerators(1, 1, b - 2)
                if exists(b - 1):
                    clamp_row_sums(b - 1)
                if exists(b - 2):
                    numerators(2, 1, b - 2)
                if exists(b - 1):
                    invert_row_sums(b - 1)
                if exists(b - 2):
                    numerators(3, 1, b - 2)
                if exists(b - 1):
                    coefficients(b - 1)
                    value_low(0, b - 1)
                    scale_gravity(b - 1)
                    mixing_sum(b - 1)
                if exists(b):
                    scale_out(0, b)
                if exists(b - 1):
                    value_low(1, b - 1)
                if exists(b - 2):
                    e_low(1, b - 2)
                if exists(b):
                    dve.wait_ge(o_relu[0], b + 1)
                    nc.vector.tensor_tensor(x_now, x_now, o_buf[:, 0, :, :], ALU.add).then_inc(x1_done, 1)
                if exists(b - 1):
                    dve.wait_ge(kt_hi, b)
                    low(k_t[1], ps_kt, k_t[0]).then_inc(kt_lo, 1)
                if exists(b):
                    dve.wait_ge(x1_done, b + 1)
                    norm_stats(1, b, x_now)
                    normalise(1, b, x_now)
                if first(b):
                    weight_low(7)
                if exists(b - 2) and exists(b):
                    scale_out(1, b - 2)
                if exists(b):
                    for half in range(2):
                        rows = slice(2 * half, 2 * half + 2)
                        dve.wait_ge(ht_hi[half], b + 1)
                        nc.vector.scalar_tensor_tensor(h_t[1][:, rows, :].rearrange("p t c -> p (t c)"),
                                                       ps_c[:, half, :], 0.0,
                                                       h_t[0][:, rows, :].bitcast(F32).rearrange("p t c -> p (t c)"),
                                                       ALU.max, ALU.subtract).then_inc(ht_lo[half], 1)
                if exists(b - 1):
                    dve.wait_ge(kp_done, b)
                    if later(b - 2):
                        dve.wait_ge(x4_done, b - 2)
                    nc.vector.tensor_tensor(x_b_last, x_other, ps_b[:, :, :], ALU.add).then_inc(x2_done, 1)
                    dve.wait_ge(x2_done, b)
                    norm_stats(2, b - 1, x_b_last)
                    normalise(2, b - 1, x_b_last)
                if exists(b - 2) and not exists(b):
                    scale_out(1, b - 2)
                if exists(b + 1):
                    next_k, next_turn = (1, turn) if k == 0 else (0, turn + 1)
                    dve.wait_ge(loaded[next_k], 16 * next_turn + 16)
                    norm_stats(0, b + 1, x_other)
                if first(b + 1):
                    first_operands()
                if exists(b - 1):
                    h_low(2, b - 1)
                if exists(b + 1):
                    normalise(0, b + 1, x_other)
                if exists(b):
                    dve.wait_ge(zl_hi, b + 1)
                    low(z_l[1][:, :, :], ps_zl, z_l[0][:, :, :]).then_inc(zl_lo, 1)
                if exists(b + 1):
                    h_low(0, b + 1)
                if exists(b):
                    dve.wait_ge(zg_hi, b + 1)
                    low(z_g[1][:, :, :], ps_zg, z_g[0][:, :, :]).then_inc(zg_lo, 1)

            constants()
            steps(dve, body)

        @block.gpsimd
        def _(pool):
            def setup():
                nc.gpsimd.memset(ident[:, :], 0.0).then_inc(setup_ident, 1)
                pool.wait_ge(setup_ident, 1)
                nc.gpsimd.affine_select(out=ident[:, :], in_=ident[:, :], compare_op=ALU.not_equal, fill=1.0,
                                        base=0, pattern=[[-1, P]], channel_multiplier=1).then_inc(setup_ident, 1)
                pool.wait_ge(setup_const, 2)

            def key_weights():
                pool.wait_ge(setup_dve, 1)
                for a in range(2):
                    for half in range(2):
                        for t in range(CT):
                            last = nc.gpsimd.tensor_copy(wk_rep[a][half][:, t, :],
                                                         wqk[half][:, a, 1, t:t + 1].bitcast(F32).to_broadcast([P, P]))
                last.then_inc(setup_ident, 1)

            def largest_query(a, e):
                pool.wait_ge(q_maxed[a], e + 1)
                if later(e):
                    pool.wait_ge(row_clamped[a], e)
                    pool.wait_ge(q_shifted[a], e)
                pool.sem_inc(pool_go, 1)
                nc.gpsimd.partition_all_reduce(q_max[:, a:a + 1], q_max1[:, a:a + 1], P, bass.bass_isa.ReduceOp.max).then_inc(q_all[a], 1)

            def e_low(a, e):
                pool.wait_ge(e_hi_01[a], e + 1)
                nc.gpsimd.tensor_tensor(e_hl[a][1][:, 0:a + 1, :], e_full[:, 0:a + 1, :],
                                        e_hl[a][0][:, 0:a + 1, :].bitcast(F32), ALU.subtract).then_inc(e_lo_01[a], 1)

            def sum_first(a, e):
                total = e_sum[:, :]
                pool.wait_ge(e_01[a], e + 1)
                other_e_used(pool, a, e, e_sum_hi)
                other_e_used(pool, a, e, e_sum_lo)
                nc.gpsimd.tensor_tensor(total, e_full[:, 0, :], e_full[:, 1, :], ALU.add).then_inc(e_part_sum[a], 1)

            def sum_rest(a, e):
                total = e_sum[:, :]
                pool.wait_ge(e_23[a], e + 1)
                pool.wait_ge(e_part_sum[a], 2 * e + 1)
                nc.gpsimd.tensor_tensor(total, total, e_full[:, 2, :], ALU.add).then_inc(e_part_sum[a], 1)
                pool.wait_ge(e_part_sum[a], 2 * e + 2)
                nc.gpsimd.tensor_tensor(total, total, e_full[:, 3, :], ALU.add).then_inc(e_summed[a], 1)

            def sum_low(a, e):
                pool.wait_ge(e_sum_hi[a], e + 1)
                other_e_used(pool, a, e, sums_done)
                nc.gpsimd.tensor_tensor(e_sum_hl[1][:, :], e_sum[:, :], e_sum_hl[0][:, :].bitcast(F32),
                                        ALU.subtract).then_inc(e_sum_lo[a], 1)

            def deviation(layer, e):
                pool.wait_ge(mean_var_done[layer], e + 1)
                if later(e):
                    pool.wait_ge(rstd_done[layer], e)
                nc.gpsimd.tensor_tensor(var_eps[:, layer, :], mean_var[:, layer, :, 1], eps_col[:, :],
                                        ALU.add).then_inc(var_eps_done[layer], 1)
                pool.wait_ge(var_eps_done[layer], e + 1)
                if later(e):
                    pool.wait_ge(norm_done[layer], e)
                nc.gpsimd.tensor_tensor(rstd[:, layer, :], var_eps[:, layer, :], mhalf_col[:, :],
                                        ALU.pow).then_inc(rstd_done[layer], 1)

            def add_input(e, k):
                pool.wait_ge(o_relu[1], e + 1)
                nc.gpsimd.tensor_tensor(o_buf[:, 1, :, :], o_buf[:, 1, :, :], x_b[:, k, :, :], ALU.add).then_inc(x4_done, 1)

            def body(b, k, turn):
                if first(b):
                    key_weights()
                if exists(b - 2):
                    deviation(3, b - 2)
                if exists(b):
                    largest_query(0, b)
                if exists(b - 1):
                    pool.wait_ge(norm_clamped, b)
                    if later(b - 1):
                        pool.wait_ge(degrees, b - 1)
                    nc.gpsimd.tensor_tensor(inv_norm, norm2, mhalf_col[:, :], ALU.pow).then_inc(norm_inv, 1)
                if exists(b):
                    sum_first(0, b)
                if exists(b - 2):
                    largest_query(1, b - 2)
                if exists(b):
                    e_low(0, b)
                    sum_rest(0, b)
                    sum_low(0, b)
                if exists(b - 2):
                    e_low(1, b - 2)
                    sum_first(1, b - 2)
                    sum_rest(1, b - 2)
                    sum_low(1, b - 2)
                if exists(b):
                    deviation(1, b)
                if exists(b - 2) and exists(b):
                    add_input(b - 2, k)
                if exists(b - 1):
                    deviation(2, b - 1)
                if exists(b + 1):
                    deviation(0, b + 1)
                if exists(b - 1):
                    pool.wait_ge(norm_done[2], b)
                    for t in range(CT):
                        last = nc.gpsimd.tensor_tensor(x_b[:, 1 - k, t, :], x_b[:, 1 - k, t, :], bias_row[:, :], ALU.add)
                    last.then_inc(x_bias, 1)
                if exists(b - 2) and not exists(b):
                    add_input(b - 2, k)

            setup()
            steps(pool, body)


_INPUTS = ["x", "adj", "L0_gnn_wq", "L0_gnn_wk", "L0_gnn_bm", "L1_gnn_W_lang", "L1_gnn_W_grav", "L1_gnn_W_V",
           "L1_gnn_W_O", "L1_gnn_gate_logit", "L1_gnn_log_sigma", "L2_gnn_bias", "L3_gnn_wq", "L3_gnn_wk", "L3_gnn_bm"]


def kernel(**inputs):
    import numpy as np
    import concourse.bacc as bacc
    from concourse.bass_utils import run_bass_kernel_spmd

    nc = bacc.Bacc("TRN2", target_bir_lowering=False, num_devices=1)
    arrays, args = {}, []
    for name in _INPUTS:
        a = np.ascontiguousarray(inputs[name])
        if a.ndim == 0:
            a = a.reshape(1)
        arrays[f"in_{name}"] = a
        args.append(nc.dram_tensor(f"in_{name}", a.shape, mybir.dt.from_np(a.dtype), kind="ExternalInput").ap())
    out = nc.dram_tensor("out", arrays["in_x"].shape, F32, kind="ExternalOutput").ap()
    emit(nc, *args, out)
    r = run_bass_kernel_spmd(nc, [arrays], core_ids=[0])
    return r.results[0]["out"]
```
